# Optimizing a Trainium2 kernel written in Bass

```python
import numpy as np
import jax
import jax.numpy as jnp

def _softmax(x, axis=-1):
    return jax.nn.softmax(x, axis=axis)

def _gelu(x):
    return jax.nn.gelu(x, approximate=True)

def _silu(x):
    return jax.nn.silu(x)

def _sigmoid(x):
    return jax.nn.sigmoid(x)

def _layernorm(x, axis=-1, eps=1e-05):
    m = jnp.mean(x, axis=axis, keepdims=True)
    v = jnp.var(x, axis=axis, keepdims=True)
    return (x - m) / jnp.sqrt(v + eps)

def _scatter_add(tgt, idx, src, axis=0):
    return tgt.at[idx].add(src)

def _segment_sum(src, seg, n):
    return jax.ops.segment_sum(src, seg, n)
kernel_name = 'mk_macaron_d1_jaxref_r8_d6e7a3'

def setup_inputs(seed: int=0):
    np.random.seed(seed)
    _w = jnp.asarray

    def _L0_attn_setup():
        import jax, jax.numpy as jnp
        import numpy as np
        C = 128
        H = 16
        K = 2
        B, N = (4, 512)

        def _heads(t):
            shp = t.shape
            d = shp[-1] // H
            t = t.reshape(shp[:-1] + (H, d))
            return jnp.swapaxes(t, -2, -3)
        key = jax.random.key(seed)
        ks_ = jax.random.split(key, 12)
        s = 1.0 / np.sqrt(C)
        inp = {'x': jax.random.normal(ks_[0], (B, N, C), dtype=jnp.float32), 'Wq': jax.random.normal(ks_[1], (C, C), dtype=jnp.float32) * s, 'bq': jnp.zeros((C,), dtype=jnp.float32), 'Wk': jax.random.normal(ks_[2], (K, C, C), dtype=jnp.float32) * s, 'bk': jnp.zeros((K, C), dtype=jnp.float32), 'Wv': jax.random.normal(ks_[3], (K, C, C), dtype=jnp.float32) * s, 'bv': jnp.zeros((K, C), dtype=jnp.float32), 'Wo': jax.random.normal(ks_[4], (C, C), dtype=jnp.float32) * s, 'bo': jnp.zeros((C,), dtype=jnp.float32), 'ln_g': jnp.ones((C,), dtype=jnp.float32), 'ln_b': jnp.zeros((C,), dtype=jnp.float32)}
        return inp
    _L0_attn_in = _L0_attn_setup()

    def _L0_ffn_setup():
        import jax, jax.numpy as jnp
        import numpy as np
        B, T, DIM = (2, 256, 128)
        H, DH, E, K = (16, 64, 8, 2)
        key = jax.random.key(seed)
        ks = jax.random.split(key, 7)
        s = 0.02
        return {'x': jax.random.normal(ks[0], (B, T, DIM), jnp.float32), 'Wq': jax.random.normal(ks[1], (H, DH, DIM), jnp.float32) * s, 'Wk': jax.random.normal(ks[2], (H, DH, DIM), jnp.float32) * s, 'Wv': jax.random.normal(ks[3], (E, DH, DIM), jnp.float32) * s, 'Ws': jax.random.normal(ks[4], (H, E, DIM), jnp.float32) * s, 'Wd': jax.random.normal(ks[5], (H, E, DIM), jnp.float32) * s, 'Wo': jax.random.normal(ks[6], (E, DIM, DH), jnp.float32) * s}
    _L0_ffn_in = _L0_ffn_setup()
    _d = {'L0_attn_x': _L0_attn_in['x'], 'L0_attn_Wq': _L0_attn_in['Wq'], 'L0_attn_bq': _L0_attn_in['bq'], 'L0_attn_Wk': _L0_attn_in['Wk'], 'L0_attn_bk': _L0_attn_in['bk'], 'L0_attn_Wv': _L0_attn_in['Wv'], 'L0_attn_bv': _L0_attn_in['bv'], 'L0_attn_Wo': _L0_attn_in['Wo'], 'L0_attn_bo': _L0_attn_in['bo'], 'L0_attn_ln_g': _L0_attn_in['ln_g'], 'L0_attn_ln_b': _L0_attn_in['ln_b'], 'L0_ffn_Wq': _L0_ffn_in['Wq'], 'L0_ffn_Wk': _L0_ffn_in['Wk'], 'L0_ffn_Wv': _L0_ffn_in['Wv'], 'L0_ffn_Ws': _L0_ffn_in['Ws'], 'L0_ffn_Wd': _L0_ffn_in['Wd'], 'L0_ffn_Wo': _L0_ffn_in['Wo']}
    _x0 = _d['L0_attn_x']
    _d['L0_attn_x'] = jax.random.normal(jax.random.fold_in(jax.random.key(seed), 1), (32, 256, 128), dtype=_x0.dtype)
    del _x0
    return _d

def reference(L0_attn_x, L0_attn_Wq, L0_attn_bq, L0_attn_Wk, L0_attn_bk, L0_attn_Wv, L0_attn_bv, L0_attn_Wo, L0_attn_bo, L0_attn_ln_g, L0_attn_ln_b, L0_ffn_Wq, L0_ffn_Wk, L0_ffn_Wv, L0_ffn_Ws, L0_ffn_Wd, L0_ffn_Wo):

    def _L0_attn_ref(x, Wq, bq, Wk, bk, Wv, bv, Wo, bo, ln_g, ln_b):
        import jax, jax.numpy as jnp
        import numpy as np
        C = 128
        H = 16
        K = 2
        B, N = (4, 512)

        def _heads(t):
            shp = t.shape
            d = shp[-1] // H
            t = t.reshape(shp[:-1] + (H, d))
            return jnp.swapaxes(t, -2, -3)
        dtype = x.dtype
        q = x + jnp.einsum('bnc,cd->bnd', x, Wq) + bq
        ks = x[None] + jnp.einsum('bnc,kcd->kbnd', x, Wk) + bk[:, None, None, :]
        vs = x[None] + jnp.einsum('bnc,kcd->kbnd', x, Wv) + bv[:, None, None, :]
        q = _heads(q)
        ks = _heads(ks)
        vs = _heads(vs)
        scale = 1.0 / jnp.sqrt(jnp.asarray(N, dtype=jnp.float32))
        ks = ks.astype(jnp.float32) * scale
        vs = vs.astype(jnp.float32) * scale
        states = jnp.einsum('kbhnd,kbhne->kbhde', ks, vs)
        state = jnp.prod(states, axis=0)
        out = jnp.einsum('bhnd,bhde->bhne', q.astype(jnp.float32), state)
        out = out.astype(dtype)
        out = jnp.swapaxes(out, 1, 2).reshape(x.shape[0], x.shape[1], C)
        mu = jnp.mean(out, axis=-1, keepdims=True)
        var = jnp.var(out, axis=-1, keepdims=True)
        out = (out - mu) / jnp.sqrt(var + 1e-05) * ln_g + ln_b
        out = jnp.einsum('bnc,cd->bnd', out, Wo) + bo
        return out

    def _L0_ffn_ref(x, Wq, Wk, Wv, Ws, Wd, Wo):
        import jax, jax.numpy as jnp
        import numpy as np
        B, T, DIM = (2, 256, 128)
        H, DH, E, K = (16, 64, 8, 2)
        scale = DH ** (-0.5)
        q = jnp.einsum('btc,hdc->bhtd', x, Wq)
        k = jnp.einsum('btc,hdc->bhtd', x, Wk)
        gate_v = jnp.einsum('btc,hec->bthe', x, Ws)
        w, sel = jax.lax.top_k(gate_v, K)
        wsig = jax.nn.sigmoid(w)
        oh = jax.nn.one_hot(sel, E, dtype=x.dtype)
        mix_v = jnp.einsum('bthk,bthke->bthe', wsig, oh)
        proj_v = jnp.einsum('btc,edc->bted', x, Wv)
        v = jnp.einsum('bthe,bted->bhtd', mix_v, proj_v)
        scores = jnp.einsum('bhid,bhjd->bhij', q * scale, k)
        probs = jax.nn.softmax(scores, axis=-1)
        attn = jnp.einsum('bhij,bhjd->bihd', probs, v)
        gate_o = jnp.einsum('btc,hec->bthe', x, Wd)
        _, sel_o = jax.lax.top_k(gate_o, K)
        mask_o = jax.nn.one_hot(sel_o, E, dtype=x.dtype).sum(axis=3)
        res = jnp.einsum('bthe,bthd,efd->bthf', mask_o, attn, Wo)
        return res.sum(axis=2)
    x = L0_attn_x
    x = x + 0.5 * _L0_ffn_ref(_layernorm(x, axis=-1), L0_ffn_Wq, L0_ffn_Wk, L0_ffn_Wv, L0_ffn_Ws, L0_ffn_Wd, L0_ffn_Wo)
    x = x + _L0_attn_ref(_layernorm(x, axis=-1), L0_attn_Wq, L0_attn_bq, L0_attn_Wk, L0_attn_bk, L0_attn_Wv, L0_attn_bv, L0_attn_Wo, L0_attn_bo, L0_attn_ln_g, L0_attn_ln_b)
    x = x + 0.5 * _L0_ffn_ref(_layernorm(x, axis=-1), L0_ffn_Wq, L0_ffn_Wk, L0_ffn_Wv, L0_ffn_Ws, L0_ffn_Wd, L0_ffn_Wo)
    return x

_drawn_inputs = setup_inputs


def setup_inputs(seed=0):
    import zlib

    import numpy as np

    out = dict(_drawn_inputs(seed))
    spreads = {'L0_attn_bq': (0.0, 0.1),
     'L0_attn_bk': (0.0, 0.614),
     'L0_attn_bv': (0.0, 0.597),
     'L0_attn_bo': (0.0, 0.1),
     'L0_attn_ln_g': (1.0, 0.2),
     'L0_attn_ln_b': (0.0, 0.1)}
    factors = {'L0_ffn_Wq': 8.0,
     'L0_ffn_Wk': 8.0,
     'L0_ffn_Wv': 4.11,
     'L0_ffn_Ws': 5.856,
     'L0_ffn_Wd': 6.32,
     'L0_ffn_Wo': 4.148}
    for name, (base, spread) in spreads.items():
        noise = np.random.default_rng([zlib.crc32(name.encode()), seed]).standard_normal(out[name].shape)
        drawn = base * np.exp(spread * noise) if base else spread * noise
        out[name] = jnp.asarray(drawn.astype(out[name].dtype))
    for name, factor in factors.items():
        out[name] = (out[name] * factor).astype(out[name].dtype)
    return out
```

```python
from contextlib import ExitStack

import concourse.bass as bass
from concourse import mybir

F32 = mybir.dt.float32
ALU = mybir.AluOpType
ACT = mybir.ActivationFunctionType
AX_X = mybir.AxisListType.X

P = 128
TK = 16
EPS = 1e-5
MISC = 3
XRING = 8
LOWEST = -3.0e38


def macaron_kernel(nc, x, WqT, WkT, WvT, WgT, WoT, aWq, aWkv, aWo, b_q, b_kv, b_o, ln_g, ln_b,
                   ident_d, delta_d, ramp_d, heads_d, out):
    NSEQ, T, C = x.shape
    NT = T // P
    E, DH = WoT.shape[1], WoT.shape[0]
    H = WqT.shape[1] // DH
    HP = H // 2
    NG = T // TK
    NP = 2 * NG
    G2 = 2 * E
    HR = P // G2
    R = H // HR
    QG = 4
    NC = NG // QG
    QSCALE = float(DH) ** -0.5
    SSCALE = (1.0 / 512.0) ** 2
    assert C == P and 2 * DH == P and TK * HP == P and TK * E == P and T == 2 * P and H == 16

    ctx = ExitStack()
    with ctx:
        def sb(name, shape):
            return ctx.enter_context(nc.sbuf_tensor(name, shape, F32))

        def pb(name, shape):
            return ctx.enter_context(nc.psum_tensor(name, shape, F32))

        ident = sb("ident", [P, P])
        delta = sb("delta", [P, TK * E])
        ramp = sb("ramp", [P, E])
        headmask = sb("headmask", [P, P])
        wq = sb("wq", [P, H * DH])
        wk = sb("wk", [P, H * DH])
        wv = sb("wv", [P, E * DH])
        wg = sb("wg", [P, H * G2])
        wo = sb("wo", [P, E, C])
        awq = sb("awq", [P, C])
        awkv = sb("awkv", [P, 4 * C])
        awo = sb("awo", [P, C])
        bq = sb("bq", [P, 1])
        bkv = sb("bkv", [P, 4 * C])
        bo = sb("bo", [P, C])
        lng = sb("lng", [P, 1])
        lnb = sb("lnb", [P, 1])
        X = sb("X", [P, XRING, NT, C])
        XN = sb("XN", [P, 2, NT, C])
        XNT = sb("XNT", [P, 2, T])
        STAT = sb("STAT", [P, 3, NT, 6])
        MV = sb("MV", [P, 3, NT, 2])
        RSTD = sb("RSTD", [P, 3, NT])
        power = sb("power", [P, NT])
        QT = sb("QT", [P, 2, HP, T])
        KT = sb("KT", [P, 2, HP, T])
        GE = sb("GE", [2 * G2, T, HP])
        GS = sb("GS", [P, NP, 2, E])
        F1 = sb("F1", [P, NP, 2, E])
        FW = sb("FW", [P, NP, 2, E])
        GM = sb("GM", [P, NP, 2, E])
        MAXV = sb("MAXV", [P, NP * 2])
        MAXR = sb("MAXR", [P, NP * 2])
        SG = sb("SG", [P, NP, E])
        MIX = sb("MIX", [P, NP, E])
        MASK = sb("MASK", [P, 2, NP, E])
        PJ = sb("PJ", [DH, T, E])
        PR = sb("PR", [P, NG, DH])
        BLK = sb("BLK", [P, NC, QG * 2, TK * E])
        BT = sb("BT", [P, 2, QG * 2, P])
        VT = sb("VT", [P, T, HP])
        V = sb("V", [P, 2, NT, HP, P])
        PB = sb("PB", [P, 3, NT, T])
        PT = sb("PT", [P, 4, NT, T])
        NMAX = sb("NMAX", [P, 3, NT])
        SUM = sb("SUM", [P, 3, NT])
        RSUM = sb("RSUM", [P, 3, NT])
        AT = sb("AT", [P, 2, T, HP])
        AN = sb("AN", [P, 2, QG, P])
        OT = sb("OT", [P, E, T])
        KV = sb("KV", [P, NT, 4 * C])
        S0 = sb("S0", [P, C])
        ST = sb("ST", [P, C])
        AQ = sb("AQ", [P, T])
        AO = sb("AO", [P, NT, C])
        AON = sb("AON", [P, NT, C])
        AOT = sb("AOT", [P, T])

        psS = [pb(f"psS{i}", [P, NT, T]) for i in range(2)]
        psT = [pb(f"psT{i}", [P, NT, T]) for i in range(2)]
        psO = pb("psO", [P, T])
        psM = [pb(f"psM{i}", [P, 512]) for i in range(MISC)]

        count, handle = {}, {}

        def sem(name):
            handle[name] = ctx.enter_context(nc.semaphore(name))
            count[name] = 0
            return name

        s_const = sem("s_const")
        s_x = [sem(f"s_x{i}") for i in range(XRING)]
        s_out = sem("s_out")
        s_dve = sem("s_dve")
        s_act = sem("s_act")
        s_pool = sem("s_pool")
        s_blk = sem("s_blk")
        s_score = sem("s_score")
        s_max = sem("s_max")
        s_exp = sem("s_exp")
        s_rsum = sem("s_rsum")
        s_norm = sem("s_norm")
        s_pt = sem("s_pt")
        s_ptc = sem("s_ptc")
        s_pv = sem("s_pv")
        s_oc = sem("s_oc")
        s_fill = [sem(f"s_fill{i}") for i in range(MISC)]
        s_free = [sem(f"s_free{i}") for i in range(MISC)]

        queue = {"pe": [], "dve": [], "act": [], "pool": [], "sp": []}
        waited = {}

        def put(engine, step, waits=(), signal=None, by=1):
            for name, value in waits:
                if value > waited.get((engine, name), 0):
                    waited[engine, name] = value
                    queue[engine].append(("wait", name, value))
            queue[engine].append(("do", step, signal, by))
            if signal is not None:
                count[signal] += by
                return signal, count[signal]

        def play(engine, eng):
            for what in queue[engine]:
                if what[0] == "wait":
                    eng.wait_ge(handle[what[1]], what[2])
                else:
                    ins = what[1](eng)
                    if what[2] is not None:
                        ins.then_inc(handle[what[2]], what[3])

        def copy(engine, dst, src, waits, signal, scale=None):
            if engine == "act":
                return put("act", lambda e: e.activation(dst, src, ACT.Copy, scale=scale or 1.0),
                           waits, signal)
            if scale is None:
                return put("dve", lambda e: e.tensor_copy(dst, src), waits, signal)
            return put("dve", lambda e: e.tensor_scalar(dst, src, scale, None, ALU.mult), waits, signal)

        bank_at = [0]
        bank_free = [[] for _ in range(MISC)]

        def fill(steps, waits):
            b = bank_at[0] % MISC
            bank_at[0] += 1
            todo = steps(psM[b])
            for n, step in enumerate(todo):
                last = n == len(todo) - 1
                full = put("pe", step, list(waits) + bank_free[b] if n == 0 else (),
                           s_fill[b] if last else None)
            return b, full

        def drain(b, full, engine, dst, src, waits=(), scale=None):
            m = copy(engine, dst, src, [full, *waits], s_free[b], scale)
            bank_free[b] = [m]
            return m

        def mm(dst, lhsT, rhs, start=True, stop=True):
            return lambda e: e.matmul(dst, lhsT, rhs, start=start, stop=stop)

        def tr(dst, src):
            k = src.shape[0]
            return lambda e: e.transpose(dst, src, ident[0:k, 0:k])

        consts = [(ident, ident_d), (delta, delta_d), (ramp, ramp_d), (headmask, heads_d), (wq, WqT),
                  (wg, WgT), (wk, WkT), (wv, WvT), (awq, aWq), (awkv, aWkv), (awo, aWo)]
        loaded_x = {}
        stored = {}

        def load_x(s):
            waits = [stored[s - XRING]] if s >= XRING else []
            loaded_x[s] = put("sp", lambda e: e.dma_start(X[:, s % XRING], x[s].rearrange("(n p) c -> p n c", p=P)),
                              waits, s_x[s % XRING], 16)

        load_x(0)
        for dst, src in consts:
            put("sp", lambda e, d=dst, s=src: e.dma_start(d[:], s), (), s_const, 16)
        for half in range(2):
            put("sp", lambda e, h=half: e.dma_start(wo[h * DH:(h + 1) * DH], WoT), (), s_const, 16)
        for dst, src in ((bq, b_q), (lng, ln_g), (lnb, ln_b)):
            put("sp", lambda e, d=dst, s=src: e.dma_start(d[:, :], s.rearrange("(p a) -> p a", a=1)), (), s_const, 16)
        for dst, src in ((bkv, b_kv), (bo, b_o)):
            put("sp", lambda e, d=dst, s=src: e.dma_start(d[:, :], s.partition_broadcast(P)), (), s_const, 16)
        const = (s_const, count[s_const])
        put("dve", lambda e: e.tensor_tensor(awq[:, :], awq[:, :], ident[:, :], ALU.add), [const], s_dve)
        for i in range(4):
            resid = put("dve", lambda e, i=i: e.tensor_tensor(awkv[:, i * C:(i + 1) * C], awkv[:, i * C:(i + 1) * C],
                                                              ident[:, :], ALU.add), [], s_dve)

        powers = put("pool", lambda e: e.memset(power[:, :], -0.5), (), s_pool)

        def layernorm(k, src, dst, ready, dst_free):
            for n in range(NT):
                m = put("dve", lambda e, n=n: e.bn_stats(STAT[:, k, n, :], src(n)), ready, s_dve)
            for n in range(NT):
                m = put("dve", lambda e, n=n: e.bn_aggr(MV[:, k, n, :], STAT[:, k, n, :]), [m], s_dve)
            yield
            m = put("pool", lambda e: e.tensor_scalar(RSTD[:, k, :], MV[:, k, :, 1], EPS, None, ALU.add), [m], s_pool)
            m = put("pool", lambda e: e.tensor_tensor(RSTD[:, k, :], RSTD[:, k, :], power[:, :], ALU.pow), [m, powers], s_pool)
            yield
            for n in range(NT):
                m2 = put("dve", lambda e, n=n: e.tensor_scalar(dst(n), src(n), MV[:, k, n, 0:1], RSTD[:, k, n:n + 1],
                                                               ALU.subtract, ALU.mult), [m, *dst_free], s_dve)
            normed[k] = m2

        normed = {}
        x_ready = {}
        free = {}
        made = {}

        def transpose_tokens(k, src, dst):
            b, full = fill(lambda M: [tr(M[:, n * P:(n + 1) * P], src(n)) for n in range(NT)], [normed[k], const])
            return b, full

        def prologue(p, s):
            o = p % 2
            if s not in loaded_x:
                load_x(s)
            ready = x_ready.get(s, [loaded_x[s]])
            yield from layernorm(0, lambda n: X[:, s % XRING, n, :], lambda n: XN[:, 0, n, :], ready, free.get("XN0", []))
            yield
            b, full = transpose_tokens(0, lambda n: XN[:, 0, n, :], None)
            free["XN0"] = [full]
            xnt = drain(b, full, "dve", XNT[:, 0, :], psM[b][:, 0:T], free.get("XNT0", []))
            yield
            b, full = fill(lambda M: [mm(M[:, r * T:(r + 1) * T], wg[:, r * P:(r + 1) * P], XNT[:, 0, :])
                                      for r in range(R)], [xnt])
            for q in range(HR // 2):
                ge = drain(b, full, "act", GE[:, :, q::HR // 2].rearrange("p t r -> p r t"),
                           psM[b][q * 2 * G2:(q + 1) * 2 * G2, :].rearrange("p (r t) -> p r t", r=R), free.get("GE", []))
            yield

            def project(kind, i):
                w, dst = (wq, QT) if kind == "q" else (wk, KT)
                b, full = fill(lambda M: [mm(M[:, j * T:(j + 1) * T], w[:, (2 * i + j) * P:(2 * i + j + 1) * P], XNT[:, 0, :])
                                          for j in range(2)], [xnt])
                free["XNT0"] = [full]
                made[kind, p, i] = drain(b, full, "act" if kind == "q" else "dve", dst[:, o, 2 * i:2 * i + 2, :],
                                         psM[b][:, :].rearrange("p (j t) -> p j t", j=2),
                                         free.get(("QK", o), []), QSCALE if kind == "q" else None)

            for i in range(2):
                b, full = fill(lambda M: [mm(M[:, j * T:(j + 1) * T], wv[:, (2 * i + j) * P:(2 * i + j + 1) * P], XNT[:, 0, :])
                                          for j in range(2)], [xnt])
                for half in range(2):
                    src = psM[b][half * DH:(half + 1) * DH, :].rearrange("p (j t) -> p j t", j=2)
                    dst = PJ[:, :, 4 * i + half:4 * i + half + 3:2].rearrange("p t j -> p j t")
                    pj = drain(b, full, ("act", "dve")[i], dst, src, free.get("PJ", []))
                yield
            for i in range(2):
                project("q", i)
                yield
                project("k", i)
                yield
            b, full = fill(lambda M: [tr(M[:, g * 2 * G2:(g + 1) * 2 * G2], GE[:, g * TK:(g + 1) * TK, :].rearrange("p t h -> p (t h)"))
                                      for g in range(NG)], [ge])
            free["GE"] = [full]
            m = drain(b, full, "act", GS[:, :, :, :].rearrange("p a b e -> p (a b e)"), psM[b][:, :], free.get("GS", []))
            gates = m
            gall, f1, fw, gm = ([t[:, :, :, :].rearrange("p a b e -> p (a b) e") for t in (GS, F1, FW, GM)])
            shape = [P, 2 * NP, E]

            def over_e(t):
                return t[:, :].unsqueeze(2).to_broadcast(shape)

            ramps = ramp[:, :].unsqueeze(1).to_broadcast(shape)
            sig = put("act", lambda e: e.activation(SG[:, :, :], GS[:, :, 0, :], ACT.Exp, scale=-1.0),
                      [m, *free.get("SG", [])], s_act)
            yield

            def pick(values, m, chosen):
                m = put("dve", lambda e: e.tensor_reduce(MAXV[:, :], values, AX_X, ALU.max), [m], s_dve)
                m = put("dve", lambda e: e.tensor_tensor(fw, values, over_e(MAXV), ALU.is_equal), [m], s_dve)
                yield
                m = put("dve", lambda e: e.tensor_tensor(fw, fw, ramps, ALU.mult), [m], s_dve)
                m = put("dve", lambda e: e.tensor_reduce(MAXR[:, :], fw, AX_X, ALU.max), [m], s_dve)
                m = put("dve", lambda e: e.tensor_tensor(chosen, fw, over_e(MAXR), ALU.is_equal), [m], s_dve)
                made["pick"] = m
                yield

            yield from pick(gall, m, f1)
            project("q", 2)
            yield
            m = put("dve", lambda e: e.scalar_tensor_tensor(gm, f1, LOWEST, gall, ALU.mult, ALU.add),
                    [made["pick"]], s_dve)
            yield from pick(gm, m, gm)
            project("k", 2)
            yield
            m = made["pick"]
            put("dve", lambda e: e.tensor_tensor(MASK[:, o, :, :], F1[:, :, 1, :], GM[:, :, 1, :], ALU.add),
                [m, *free.get(("MASK", o), [])], s_dve)
            m = put("dve", lambda e: e.tensor_tensor(MIX[:, :, :], F1[:, :, 0, :], GM[:, :, 0, :], ALU.add),
                    free.get("MIX", []), s_dve)
            made["MASK", p] = m
            m2 = put("dve", lambda e: e.tensor_scalar(SG[:, :, :], SG[:, :, :], 1.0, None, ALU.add), [sig], s_dve)
            m2 = put("dve", lambda e: e.reciprocal(SG[:, :, :], SG[:, :, :]), [m2], s_dve)
            m = put("dve", lambda e: e.tensor_tensor(MIX[:, :, :], MIX[:, :, :], SG[:, :, :], ALU.mult), [m2], s_dve)
            free["SG"] = [m]
            free["GS"] = [m]
            mix = m
            for i in range(2):
                half = NG // 2
                b, full = fill(lambda M: [tr(M[:, g * DH:(g + 1) * DH],
                                             PJ[:, (i * half + g) * TK:(i * half + g + 1) * TK, :].rearrange("d t e -> d (t e)"))
                                          for g in range(half)], [pj])
                pr = drain(b, full, "act", PR[:, i * half:(i + 1) * half, :],
                           psM[b][:, :].rearrange("p (g d) -> p g d", d=DH), free.get("PR", []))
                yield
            free["PJ"] = [full]
            project("q", 3)
            yield
            project("k", 3)
            yield
            blk = []
            for c in range(NC):
                blk.append(blocks(c, MIX[:, c * QG * 2:(c + 1) * QG * 2, :], mix))
            free["MIX"] = [blk[-1]]
            bt = [None] * NC
            for c in range(NC + 1):
                if c < NC:
                    for i in range(2):
                        b, full = fill(lambda M: [tr(M[:, j * P:(j + 1) * P], BLK[:, c, 4 * i + j, :]) for j in range(4)],
                                       [blk[c]])
                        bt[c] = drain(b, full, ("act", "dve")[i], BT[:, c % 2, 4 * i:4 * i + 4, :],
                                      psM[b][:, :].rearrange("p (j t) -> p j t", j=4), free.get(("BT", c % 2), []))
                        made["BT", c, i] = bt[c]
                        yield
                    free["BLK", c] = [full]
                if c > 0:
                    a = c - 1
                    def mix_steps(M):
                        return [mm(M[par * DH:(par + 1) * DH, g * P:(g + 1) * P], PR[:, a * QG + g, :],
                                   BT[:, a % 2, 2 * g + par, :]) for g in range(QG) for par in range(2)]
                    b, full = fill(mix_steps, [made["BT", a, 0], made["BT", a, 1], pr])
                    free["BT", a % 2] = [full]
                    free["PR"] = [full]
                    vt = drain(b, full, ("act", "dve")[a % 2], VT[:, a * QG * TK:(a + 1) * QG * TK, :],
                               psM[b][:, :].rearrange("p (t h) -> p t h", h=HP), free.get("VT", []))
                    made["VT", a] = vt
                    yield
            for i in range(4):
                jt, hp0 = i // 2, 4 * (i % 2)
                b, full = fill(lambda M: [tr(M[:, j * P:(j + 1) * P], VT[:, jt * P:(jt + 1) * P, hp0 + j]) for j in range(4)],
                               [made["VT", a] for a in range(NC)])
                made["V", p, i] = drain(b, full, ("act", "dve")[i % 2], V[:, o, jt, hp0:hp0 + 4, :],
                                        psM[b][:, :].rearrange("p (j t) -> p j t", j=4), free.get(("V", o), []))
                yield
            free["VT"] = [full]

        def blocks(c, gates, ready):
            shape = [P, QG * 2, TK, E]
            dst = BLK[:, c, :, :].rearrange("p a (t e) -> p a t e", e=E)
            g4 = gates.unsqueeze(2).to_broadcast(shape)
            d4 = delta[:, :].rearrange("p (t e) -> p t e", e=E).unsqueeze(1).to_broadcast(shape)
            return put("pool", lambda e: e.tensor_tensor(dst, g4, d4, ALU.mult),
                       [ready, const, *free.get(("BLK", c), [])], s_blk)

        def epilogue(p, s, attention):
            o = p % 2
            blk = [blocks(c, MASK[:, o, c * QG * 2:(c + 1) * QG * 2, :], made["MASK", p]) for c in range(NC)]
            free["MASK", o] = [blk[-1]]
            an = [None] * NC
            for c in range(NC + 1):
                if c < NC:
                    b, full = fill(lambda M: [tr(M[:, j * P:(j + 1) * P],
                                                 AT[:, o, (c * QG + j) * TK:(c * QG + j + 1) * TK, :].rearrange("p t h -> p (t h)"))
                                              for j in range(QG)], [made["AT", p]])
                    an[c] = drain(b, full, ("act", "dve")[c % 2], AN[:, c % 2, :, :],
                                  psM[b][:, :].rearrange("p (j t) -> p j t", j=QG), free.get(("AN", c % 2), []))
                    if c == NC - 1:
                        free["AT", o] = [full]
                    yield
                if c > 0:
                    a = c - 1
                    b, full = fill(lambda M: [mm(M[par * DH:(par + 1) * DH, g * P:(g + 1) * P],
                                                 AN[:, a % 2, g, par * DH:(par + 1) * DH], BLK[:, a, 2 * g + par, :])
                                              for g in range(QG) for par in range(2)], [an[a], blk[a]])
                    free["AN", a % 2] = [full]
                    free["BLK", a] = [full]
                    n = QG * TK
                    made["OT", a] = drain(b, full, ("act", "dve")[a % 2],
                                          OT[:, :, a * n:(a + 1) * n].rearrange("p e t -> p t e"),
                                          psM[b][:, :].rearrange("p (t e) -> p t e", e=E), free.get("OT", []))
                    yield
            b, full = fill(lambda M: [mm(M[:, n * C:(n + 1) * C], OT[:, e, n * P:(n + 1) * P], wo[:, e, :], e == 0, e == E - 1)
                                      for n in range(NT) for e in range(E)], [made["OT", a] for a in range(NC)])
            free["OT"] = [full]
            xs = X[:, s % XRING, :, :].rearrange("p n c -> p (n c)")
            m = put("dve", lambda e, b=b: e.scalar_tensor_tensor(xs, psM[b][:, 0:NT * C], 0.5, xs, ALU.mult, ALU.add),
                    [full], s_free[b])
            bank_free[b] = [m]
            x_ready[s] = [m]
            yield
            if not attention:
                stored[s] = put("sp", lambda e: e.dma_start(out[s].rearrange("(n p) c -> p n c", p=P), X[:, s % XRING]),
                                [m], s_out, 16)
                return
            yield from layernorm(1, lambda n: X[:, s % XRING, n, :], lambda n: XN[:, 1, n, :], [m], free.get("XN1", []))
            yield
            b, full = transpose_tokens(1, lambda n: XN[:, 1, n, :], None)
            free["XN1"] = [full]
            xnt = drain(b, full, "act", XNT[:, 1, :], psM[b][:, 0:T], free.get("XNT1", []))
            yield
            for n in range(NT):
                b, full = fill(lambda M: [mm(M[:, :], XNT[:, 1, n * P:(n + 1) * P], awkv[:, :])], [xnt, resid])
                kv = put("dve", lambda e, b=b, n=n: e.tensor_tensor(KV[:, n, :], psM[b][:, :], bkv[:, :], ALU.add),
                         [full, *free.get("KV", [])], s_free[b])
                bank_free[b] = [kv]
                yield
            b, full = fill(lambda M: [mm(M[:, 0:T], awq[:, :], XNT[:, 1, :])], [xnt, resid])
            free["XNT1"] = [full]
            aq = put("dve", lambda e, b=b: e.tensor_scalar(AQ[:, :], psM[b][:, 0:T], bq[:, 0:1], None, ALU.add),
                     [full, *free.get("AQ", [])], s_free[b])
            bank_free[b] = [aq]
            yield
            b, full = fill(lambda M: [mm(M[:, k * C:(k + 1) * C], KV[:, n, k * C:(k + 1) * C], KV[:, n, (2 + k) * C:(3 + k) * C],
                                         n == 0, n == NT - 1) for k in range(2) for n in range(NT)], [kv])
            free["KV"] = [full]
            m = put("dve", lambda e, b=b: e.scalar_tensor_tensor(S0[:, :], psM[b][:, 0:C], SSCALE, headmask[:, :],
                                                                 ALU.mult, ALU.mult), [full], s_dve)
            m = put("dve", lambda e, b=b: e.tensor_tensor(ST[:, :], psM[b][:, C:2 * C], S0[:, :], ALU.mult),
                    [m, *free.get("ST", [])], s_free[b])
            bank_free[b] = [m]
            yield
            b, full = fill(lambda M: [mm(M[:, n * C:(n + 1) * C], AQ[:, n * P:(n + 1) * P], ST[:, :]) for n in range(NT)],
                           [aq, m])
            free["ST"] = free["AQ"] = [full]
            m = drain(b, full, "act", AO[:, :, :], psM[b][:, 0:NT * C].rearrange("p (n c) -> p n c", n=NT),
                      free.get("AO", []))
            yield
            yield from layernorm(2, lambda n: AO[:, n, :], lambda n: AON[:, n, :], [m], free.get("AON", []))
            free["AO"] = [normed[2]]
            yield
            b, full = transpose_tokens(2, lambda n: AON[:, n, :], None)
            free["AON"] = [full]
            m = put("dve", lambda e, b=b: e.tensor_scalar(AOT[:, :], psM[b][:, 0:T], lng[:, 0:1], lnb[:, 0:1], ALU.mult, ALU.add),
                    [full, *free.get("AOT", [])], s_free[b])
            bank_free[b] = [m]
            yield
            b, full = fill(lambda M: [mm(M[:, n * C:(n + 1) * C], AOT[:, n * P:(n + 1) * P], awo[:, :]) for n in range(NT)], [m])
            free["AOT"] = [full]
            m = put("dve", lambda e, b=b: e.tensor_tensor(xs, psM[b][:, 0:NT * C], xs, ALU.add), [full], s_free[b])
            bank_free[b] = [m]
            xn = X[:, s % XRING, :, :]
            m = put("pool", lambda e: e.tensor_tensor(xn, xn, bo[:, :].unsqueeze(1).to_broadcast([P, NT, C]), ALU.add),
                    [m], s_pool)
            x_ready[s] = [m]

        score_free = [[], []]
        pt_free = [[], []]
        o_free = []
        pb_free = [[], [], []]
        ptb_free = [[] for _ in range(4)]
        normed_head, copied = {}, {}

        def scores(n):
            p, h = divmod(n, H)
            o, hp, par, r = p % 2, h // 2, h % 2, n % 3
            lo = par * DH
            for it in range(NT):
                m = put("pe", mm(psS[n % 2][:, it, :], QT[lo:lo + DH, o, hp, it * P:(it + 1) * P], KT[lo:lo + DH, o, hp, :]),
                        [made["q", p, hp // 2], made["k", p, hp // 2], *score_free[n % 2]] if it == 0 else (),
                        s_score if it == NT - 1 else None)
            if h == H - 1:
                free["QK", o] = [m]
            m = put("dve", lambda e: e.tensor_reduce(NMAX[:, r, :], psS[n % 2][:, :, :], AX_X, ALU.max, negate=True),
                    [m], s_max)
            for it in range(NT):
                m2 = put("act", lambda e, it=it: e.activation(PB[:, r, it, :], psS[n % 2][:, it, :], ACT.Exp,
                                                             bias=NMAX[:, r, it:it + 1], accum_out=SUM[:, r, it:it + 1]),
                         [m, *pb_free[r]], s_exp)
            score_free[n % 2] = [m2]
            m = put("dve", lambda e: e.reciprocal(RSUM[:, r, :], SUM[:, r, :]), [m2], s_rsum)
            for it in range(NT):
                m2 = put("pool", lambda e, it=it: e.tensor_scalar(PB[:, r, it, :], PB[:, r, it, :], RSUM[:, r, it:it + 1],
                                                                 None, ALU.mult), [m], s_norm)
            normed_head[n] = m2

        def turn(n):
            r = n % 3
            steps = [tr(psT[n % 2][:, jt, it * P:(it + 1) * P], PB[:, r, it, jt * P:(jt + 1) * P])
                     for it in range(NT) for jt in range(NT)]
            for k, step in enumerate(steps):
                m = put("pe", step, [normed_head[n], *pt_free[n % 2]] if k == 0 else (), s_pt if k == 3 else None)
            pb_free[r] = [m]
            m = put("dve", lambda e: e.tensor_copy(PT[:, n % 4, :, :], psT[n % 2][:, :, :]), [m, *ptb_free[n % 4]], s_ptc)
            pt_free[n % 2] = [m]
            copied[n] = m

        def product(n):
            p, h = divmod(n, H)
            o, hp = p % 2, h // 2
            vs = [made["V", p, 2 * jt + hp // 4] for jt in range(NT)]
            for jt in range(NT):
                for par in range(2):
                    first = jt == par == 0
                    last = jt == NT - 1 and par == 1
                    m = put("pe", mm(psO[par * DH:(par + 1) * DH, :], V[:, o, jt, hp, par * DH:(par + 1) * DH],
                                     PT[:, (n + par) % 4, jt, :], jt == 0, jt == NT - 1),
                            [copied[n], copied[n + 1], *vs, *o_free] if first else (), s_pv if last else None)
            ptb_free[n % 4] = ptb_free[(n + 1) % 4] = [m]
            if h == H - 2:
                free["V", o] = [m]
            m = put("act", lambda e: e.activation(AT[:, o, :, hp], psO[:, :], ACT.Copy), [m, *free.get(("AT", o), [])], s_oc)
            o_free[:] = [m]
            made["AT", p] = m

        LEAD = 3
        order = [(s, True) for s in range(min(LEAD, NSEQ))]
        for s in range(NSEQ):
            order.append((s, False))
            if s + LEAD < NSEQ:
                order.append((s + LEAD, True))
        if NSEQ < LEAD:
            raise ValueError("too few sequences")

        for _ in prologue(0, order[0][0]):
            pass
        scores(0)
        total = len(order) * H
        work = []
        for n in range(total + 3):
            p, h = divmod(n, H)
            if h == 0 and p + 1 < len(order):
                work.append([prologue(p + 1, order[p + 1][0]), H - 1])
            if h == 2 and 0 < p <= len(order):
                work.append([epilogue(p - 1, *order[p - 1]), H - 1])
            if n + 1 < total:
                if (n + 1) % H == 0:
                    for w in work:
                        for _ in w[0]:
                            pass
                    work = []
                scores(n + 1)
            for turn_of in range(3):
                for w in list(work):
                    if turn_of < 2 or w[1] and h % 2:
                        if next(w[0], StopIteration) is StopIteration:
                            work.remove(w)
            if 1 <= n <= total:
                turn(n - 1)
            if n >= 3 and (n - 3) % 2 == 0 and n - 3 < total:
                product(n - 3)
        for w in work:
            for _ in w[0]:
                pass
        work = [epilogue(len(order) - 1, *order[-1])] if (total + 2) % H < 2 else []
        for w in work:
            for _ in w:
                pass
        queue["sp"].append(("wait", s_out, count[s_out]))

        block = ctx.enter_context(nc.Block())

        @block.sync
        def _(eng):
            play("sp", eng)

        @block.tensor
        def _(eng):
            play("pe", eng)

        @block.vector
        def _(eng):
            play("dve", eng)

        @block.scalar
        def _(eng):
            play("act", eng)

        @block.gpsimd
        def _(eng):
            play("pool", eng)


def kernel(**inputs):
    import numpy as np
    import concourse.bacc as bacc
    from concourse.bass_utils import run_bass_kernel_spmd

    a = {k: np.asarray(v) for k, v in inputs.items()}
    x = a["L0_attn_x"]
    n, t, c = x.shape
    h, dh = a["L0_ffn_Wq"].shape[:2]
    e = a["L0_ffn_Wv"].shape[0]
    head = 8
    one = np.float32(1)
    row, col = np.arange(P)[:, None], np.arange(P)[None, :]
    arrays = {
        "x": x,
        "WqT": a["L0_ffn_Wq"].reshape(h * dh, c).T,
        "WkT": a["L0_ffn_Wk"].reshape(h * dh, c).T,
        "WvT": a["L0_ffn_Wv"].reshape(e * dh, c).T,
        "WgT": np.concatenate([a["L0_ffn_Ws"], a["L0_ffn_Wd"]], axis=1).reshape(h * 2 * e, c).T,
        "WoT": a["L0_ffn_Wo"].transpose(2, 0, 1),
        "aWq": a["L0_attn_Wq"],
        "aWkv": np.concatenate([*a["L0_attn_Wk"], *a["L0_attn_Wv"]], axis=1),
        "aWo": a["L0_attn_Wo"],
        "b_q": a["L0_attn_bq"],
        "b_kv": np.concatenate([*a["L0_attn_bk"], *a["L0_attn_bv"]]),
        "b_o": a["L0_attn_bo"],
        "ln_g": a["L0_attn_ln_g"],
        "ln_b": a["L0_attn_ln_b"],
        "ident": np.where(row == col, one, 0 * one),
        "delta": np.where(row // 8 == col // 8, one, 0 * one),
        "ramp": np.broadcast_to(np.arange(e, 0, -1, dtype=np.float32), (P, e)),
        "heads": np.where(row // head == col // head, one, 0 * one),
    }
    arrays = {k: np.ascontiguousarray(v) for k, v in arrays.items()}
    nc = bacc.Bacc("TRN2", target_bir_lowering=False, num_devices=1)
    args = [nc.dram_tensor(f"in_{k}", v.shape, mybir.dt.from_np(v.dtype), kind="ExternalInput").ap()
            for k, v in arrays.items()]
    out = nc.dram_tensor("out", x.shape, F32, kind="ExternalOutput").ap()
    macaron_kernel(nc, *args, out)
    r = run_bass_kernel_spmd(nc, [{f"in_{k}": v for k, v in arrays.items()}], core_ids=[0])
    return r.results[0]["out"]
```

```python
from contextlib import ExitStack

import concourse.bass as bass
from concourse import mybir

F32 = mybir.dt.float32
ALU = mybir.AluOpType
ACT = mybir.ActivationFunctionType
AX_X = mybir.AxisListType.X

P = 128
TK = 16
EPS = 1e-5
MISC = 3
XRING = 8
LOWEST = -3.0e38


def macaron_kernel(nc, x, WqT, WkT, WvT, WgT, WoT, aWq, aWkv, aWo, b_q, b_kv, b_o, ln_g, ln_b,
                   ident_d, order_d, delta_d, ramp_d, heads_d, out):
    NSEQ, T, C = x.shape
    NT = T // P
    E, DH = WoT.shape[1], WoT.shape[0]
    H = WqT.shape[1] // DH
    HP = H // 2
    NG = T // TK
    NP = 2 * NG
    G2 = 2 * E
    HR = P // G2
    R = H // HR
    QG = 4
    NC = NG // QG
    QSCALE = float(DH) ** -0.5
    SSCALE = (1.0 / 512.0) ** 2
    assert C == P and 2 * DH == P and TK * HP == P and TK * E == P and T == 2 * P and H == 16

    ctx = ExitStack()
    with ctx:
        def sb(name, shape):
            return ctx.enter_context(nc.sbuf_tensor(name, shape, F32))

        def pb(name, shape):
            return ctx.enter_context(nc.psum_tensor(name, shape, F32))

        ident = sb("ident", [P, P])
        keyorder = sb("keyorder", [P, P])
        delta = sb("delta", [P, TK * E])
        ramp = sb("ramp", [P, E])
        headmask = sb("headmask", [P, P])
        wq = sb("wq", [P, H * DH])
        wk = sb("wk", [P, H * DH])
        wv = sb("wv", [P, E * DH])
        wg = sb("wg", [P, H * G2])
        wo = sb("wo", [P, E, C])
        awq = sb("awq", [P, C])
        awkv = sb("awkv", [P, 4 * C])
        awo = sb("awo", [P, C])
        bq = sb("bq", [P, 1])
        bkv = sb("bkv", [P, 4 * C])
        bo = sb("bo", [P, C])
        lng = sb("lng", [P, 1])
        lnb = sb("lnb", [P, 1])
        X = sb("X", [P, XRING, NT, C])
        XN = sb("XN", [P, 2, NT, C])
        XNT = sb("XNT", [P, 2, T])
        XKT = sb("XKT", [P, T])
        STAT = sb("STAT", [P, 3, NT, 6])
        MV = sb("MV", [P, 3, NT, 2])
        RSTD = sb("RSTD", [P, 3, NT])
        power = sb("power", [P, NT])
        QT = sb("QT", [P, 2, HP, T])
        KT = sb("KT", [P, 2, HP, T])
        GE = sb("GE", [2 * G2, T, HP])
        GS = sb("GS", [P, NP, 2, E])
        F1 = sb("F1", [P, NP, 2, E])
        FW = sb("FW", [P, NP, 2, E])
        GM = sb("GM", [P, NP, 2, E])
        MAXV = sb("MAXV", [P, NP * 2])
        MAXR = sb("MAXR", [P, NP * 2])
        SG = sb("SG", [P, NP, E])
        MIX = sb("MIX", [P, 2, NG, E])
        MASK = sb("MASK", [P, 2, NP, E])
        PJ = sb("PJ", [DH, T, E])
        PR = sb("PR", [P, NG, DH])
        BLK = sb("BLK", [P, NC, QG * 2, TK * E])
        MT = sb("MT", [P, 2, NC, QG * HP])
        BT = sb("BT", [P, 2, 2, QG, P])
        VT = sb("VT", [P, T, HP])
        V = sb("V", [P, 2, NT, HP, P])
        PB = sb("PB", [P, 3, NT, T])
        PT = sb("PT", [P, 4, NT, T])
        NMAX = sb("NMAX", [P, 3, NT])
        SUM = sb("SUM", [P, 3, NT])
        RSUM = sb("RSUM", [P, 3, NT])
        AT = sb("AT", [P, 2, T, HP])
        AN = sb("AN", [P, 2, QG, P])
        OT = sb("OT", [P, E, T])
        KV = sb("KV", [P, NT, 4 * C])
        S0 = sb("S0", [P, C])
        ST = sb("ST", [P, C])
        AQ = sb("AQ", [P, T])
        AO = sb("AO", [P, NT, C])
        AON = sb("AON", [P, NT, C])
        AOT = sb("AOT", [P, T])

        psS = [pb(f"psS{i}", [P, NT, T]) for i in range(2)]
        psT = [pb(f"psT{i}", [P, NT, T]) for i in range(2)]
        psO = pb("psO", [P, T])
        psM = [pb(f"psM{i}", [P, 512]) for i in range(MISC)]

        count, handle = {}, {}

        def sem(name):
            handle[name] = ctx.enter_context(nc.semaphore(name))
            count[name] = 0
            return name

        s_const = sem("s_const")
        s_x = [sem(f"s_x{i}") for i in range(XRING)]
        s_out = sem("s_out")
        s_dve = sem("s_dve")
        s_act = sem("s_act")
        s_pool = sem("s_pool")
        s_blk = sem("s_blk")
        s_score = sem("s_score")
        s_max = sem("s_max")
        s_exp = sem("s_exp")
        s_rsum = sem("s_rsum")
        s_norm = sem("s_norm")
        s_pt = sem("s_pt")
        s_ptc = sem("s_ptc")
        s_pv = sem("s_pv")
        s_oc = sem("s_oc")
        s_fill = [sem(f"s_fill{i}") for i in range(MISC)]
        s_free = [sem(f"s_free{i}") for i in range(MISC)]

        queue = {"pe": [], "dve": [], "act": [], "pool": [], "sp": []}
        waited = {}

        def put(engine, step, waits=(), signal=None, by=1):
            for name, value in waits:
                if value > waited.get((engine, name), 0):
                    waited[engine, name] = value
                    queue[engine].append(("wait", name, value))
            queue[engine].append(("do", step, signal, by))
            if signal is not None:
                count[signal] += by
                return signal, count[signal]

        def play(engine, eng):
            for what in queue[engine]:
                if what[0] == "wait":
                    eng.wait_ge(handle[what[1]], what[2])
                else:
                    ins = what[1](eng)
                    if what[2] is not None:
                        ins.then_inc(handle[what[2]], what[3])

        def copy(engine, dst, src, waits, signal, scale=None):
            if engine == "act":
                return put("act", lambda e: e.activation(dst, src, ACT.Copy, scale=scale or 1.0),
                           waits, signal)
            if scale is None:
                return put("dve", lambda e: e.tensor_copy(dst, src), waits, signal)
            return put("dve", lambda e: e.tensor_scalar(dst, src, scale, None, ALU.mult), waits, signal)

        bank_at = [0]
        bank_free = [[] for _ in range(MISC)]

        def fill(steps, waits):
            b = bank_at[0] % MISC
            bank_at[0] += 1
            todo = steps(psM[b])
            for n, step in enumerate(todo):
                last = n == len(todo) - 1
                full = put("pe", step, list(waits) + bank_free[b] if n == 0 else (),
                           s_fill[b] if last else None)
            return b, full

        def drain(b, full, engine, dst, src, waits=(), scale=None):
            m = copy(engine, dst, src, [full, *waits], s_free[b], scale)
            bank_free[b] = [m]
            return m

        load = [0.0]

        def mm(dst, lhsT, rhs, start=True, stop=True):
            columns = max(64, rhs.free_size()) * (1 if lhsT.free_size() > DH else 0.5)
            load[0] += 4 * columns / 2400
            return lambda e: e.matmul(dst, lhsT, rhs, start=start, stop=stop)

        def tr(dst, src):
            k = src.shape[0]
            load[0] += 2 * P / 2400
            return lambda e: e.transpose(dst, src, ident[0:k, 0:k])

        consts = [(ident, ident_d), (keyorder, order_d), (delta, delta_d), (ramp, ramp_d), (headmask, heads_d), (wq, WqT),
                  (wg, WgT), (wk, WkT), (wv, WvT), (awq, aWq), (awkv, aWkv), (awo, aWo)]
        loaded_x = {}
        stored = {}

        def load_x(s):
            waits = [stored[s - XRING]] if s >= XRING else []
            loaded_x[s] = put("sp", lambda e: e.dma_start(X[:, s % XRING], x[s].rearrange("(n p) c -> p n c", p=P)),
                              waits, s_x[s % XRING], 16)

        load_x(0)
        for dst, src in consts:
            put("sp", lambda e, d=dst, s=src: e.dma_start(d[:], s), (), s_const, 16)
        for half in range(2):
            put("sp", lambda e, h=half: e.dma_start(wo[h * DH:(h + 1) * DH], WoT), (), s_const, 16)
        for dst, src in ((bq, b_q), (lng, ln_g), (lnb, ln_b)):
            put("sp", lambda e, d=dst, s=src: e.dma_start(d[:, :], s.rearrange("(p a) -> p a", a=1)), (), s_const, 16)
        for dst, src in ((bkv, b_kv), (bo, b_o)):
            put("sp", lambda e, d=dst, s=src: e.dma_start(d[:, :], s.partition_broadcast(P)), (), s_const, 16)
        const = (s_const, count[s_const])
        put("dve", lambda e: e.tensor_tensor(awq[:, :], awq[:, :], ident[:, :], ALU.add), [const], s_dve)
        for i in range(4):
            resid = put("dve", lambda e, i=i: e.tensor_tensor(awkv[:, i * C:(i + 1) * C], awkv[:, i * C:(i + 1) * C],
                                                              ident[:, :], ALU.add), [], s_dve)

        powers = put("pool", lambda e: e.memset(power[:, :], -0.5), (), s_pool)

        def layernorm(k, src, dst, ready, dst_free):
            for n in range(NT):
                m = put("dve", lambda e, n=n: e.bn_stats(STAT[:, k, n, :], src(n)), ready, s_dve)
            for n in range(NT):
                m = put("dve", lambda e, n=n: e.bn_aggr(MV[:, k, n, :], STAT[:, k, n, :]), [m], s_dve)
            yield
            m = put("pool", lambda e: e.tensor_scalar(RSTD[:, k, :], MV[:, k, :, 1], EPS, None, ALU.add), [m], s_pool)
            m = put("pool", lambda e: e.tensor_tensor(RSTD[:, k, :], RSTD[:, k, :], power[:, :], ALU.pow), [m, powers], s_pool)
            yield
            for n in range(NT):
                m2 = put("dve", lambda e, n=n: e.tensor_scalar(dst(n), src(n), MV[:, k, n, 0:1], RSTD[:, k, n:n + 1],
                                                               ALU.subtract, ALU.mult), [m, *dst_free], s_dve)
            normed[k] = m2

        normed = {}
        x_ready = {}
        free = {}
        made = {}

        def transpose_tokens(k, src, dst):
            b, full = fill(lambda M: [tr(M[:, n * P:(n + 1) * P], src(n)) for n in range(NT)], [normed[k], const])
            return b, full

        stages = []
        clock = [0.0]

        sizes = {}

        class Background:
            LIGHT = 0.1

            def __init__(self, steps, kind, start, end):
                self.steps, self.kind, self.start, self.end = steps, kind, start, end
                self.size, self.at, self.done = sizes.get(kind, 20.0), 0.0, False

            def step(self):
                before = load[0]
                if next(self.steps, "end") == "end":
                    self.done = True
                    sizes[self.kind] = self.at
                self.at += load[0] - before + self.LIGHT

            def due(self, now):
                goal = self.size * (now - self.start) / (self.end - self.start)
                return not self.done and self.at < goal

            def finish(self):
                while not self.done:
                    self.step()

        def choose(p, m):
            o = p % 2
            gall, f1, fw, gm = ([t[:, :, :, :].rearrange("p a b e -> p (a b) e") for t in (GS, F1, FW, GM)])
            shape = [P, 2 * NP, E]

            def over_e(t):
                return t[:, :].unsqueeze(2).to_broadcast(shape)

            ramps = ramp[:, :].unsqueeze(1).to_broadcast(shape)
            sig = put("act", lambda e: e.activation(SG[:, :, :], GS[:, :, 0, :], ACT.Exp, scale=-1.0),
                      [m, *free.get("SG", [])], s_act)
            yield

            def pick(values, m, chosen):
                m = put("dve", lambda e: e.tensor_reduce(MAXV[:, :], values, AX_X, ALU.max), [m], s_dve)
                yield
                m = put("dve", lambda e: e.tensor_tensor(fw, values, over_e(MAXV), ALU.is_equal), [m], s_dve)
                yield
                m = put("dve", lambda e: e.tensor_tensor(fw, fw, ramps, ALU.mult), [m], s_dve)
                yield
                m = put("dve", lambda e: e.tensor_reduce(MAXR[:, :], fw, AX_X, ALU.max), [m], s_dve)
                yield
                m = put("dve", lambda e: e.tensor_tensor(chosen, fw, over_e(MAXR), ALU.is_equal), [m], s_dve)
                made["pick"] = m
                yield

            yield from pick(gall, m, f1)
            m = put("dve", lambda e: e.scalar_tensor_tensor(gm, f1, LOWEST, gall, ALU.mult, ALU.add),
                    [made["pick"]], s_dve)
            yield from pick(gm, m, gm)
            m = made["pick"]
            put("dve", lambda e: e.tensor_tensor(MASK[:, o, :, :], F1[:, :, 1, :], GM[:, :, 1, :], ALU.add),
                [m, *free.get(("MASK", o), [])], s_dve)
            made["MASK", p] = (s_dve, count[s_dve])
            m = put("dve", lambda e: e.tensor_tensor(F1[:, :, 0, :], F1[:, :, 0, :], GM[:, :, 0, :], ALU.add), [m], s_dve)
            yield
            m2 = put("dve", lambda e: e.tensor_scalar(SG[:, :, :], SG[:, :, :], 1.0, None, ALU.add), [sig], s_dve)
            m2 = put("dve", lambda e: e.reciprocal(SG[:, :, :], SG[:, :, :]), [m2, m], s_dve)
            yield
            m = put("dve", lambda e: e.tensor_tensor(MIX[:, :, :, :].rearrange("p a g e -> p g a e"),
                                                     F1[:, :, 0, :].rearrange("p (g a) e -> p g a e", a=2),
                                                     SG[:, :, :].rearrange("p (g a) e -> p g a e", a=2), ALU.mult),
                    [m2], s_dve)
            free["SG"] = [m]
            free["GS"] = [m]
            yield
            mt = put("dve", lambda e: e.transpose(MT[:, :, :, :].rearrange("p a b c -> p (a b c)"),
                                                  MIX[:, :, :, :].rearrange("p a g e -> p (a g e)")),
                     [m, *free.get("MT", [])], s_dve)
            made["MT", p] = mt
            yield
            made["BT", p] = [value_blocks(c, mt) for c in range(2)]

        def norm(p, s):
            if s not in loaded_x:
                load_x(s)
            ready = x_ready.get(s, [loaded_x[s]])
            yield from layernorm(0, lambda n: X[:, s % XRING, n, :], lambda n: XN[:, 0, n, :], ready, free.get("XN0", []))

        def prologue(p, s):
            o = p % 2
            b, full = transpose_tokens(0, lambda n: XN[:, 0, n, :], None)
            free["XN0"] = [full]
            xnt = drain(b, full, "act", XNT[:, 0, :], psM[b][:, 0:T], free.get("XNT0", []))
            b, full = fill(lambda M: [(lambda e, n=n: e.transpose(M[:, n * P:(n + 1) * P], XN[:, 0, n, :], keyorder[:, :]))
                                      for n in range(NT)], [normed[0], const])
            free["XN0"] = [full]
            xkt = drain(b, full, "dve", XKT[:, :], psM[b][:, 0:T], free.get("XKT", []))
            yield
            b, full = fill(lambda M: [mm(M[:, r * T:(r + 1) * T], wg[:, r * P:(r + 1) * P], XNT[:, 0, :])
                                      for r in range(R)], [xnt])
            for q in range(HR // 2):
                ge = drain(b, full, "act", GE[:, :, q::HR // 2].rearrange("p t r -> p r t"),
                           psM[b][q * 2 * G2:(q + 1) * 2 * G2, :].rearrange("p (r t) -> p r t", r=R), free.get("GE", []))
            yield

            def project(kind, i):
                w, dst, xt = (wq, QT, XNT[:, 0, :]) if kind == "q" else (wk, KT, XKT[:, :])
                b, full = fill(lambda M: [mm(M[:, j * T:(j + 1) * T], w[:, (2 * i + j) * P:(2 * i + j + 1) * P], xt)
                                          for j in range(2)], [xnt, xkt])
                free["XNT0" if kind == "q" else "XKT"] = [full]
                made[kind, p, i] = drain(b, full, "act" if kind == "q" else "dve", dst[:, o, 2 * i:2 * i + 2, :],
                                         psM[b][:, :].rearrange("p (j t) -> p j t", j=2),
                                         free.get(("QK", o), []), QSCALE if kind == "q" else None)

            pj = []
            for i in range(2):
                b, full = fill(lambda M: [mm(M[:, j * T:(j + 1) * T], wv[:, (2 * i + j) * P:(2 * i + j + 1) * P], XKT[:, :])
                                          for j in range(2)], [xkt])
                for half in range(2):
                    src = psM[b][half * DH:(half + 1) * DH, :].rearrange("p (j t) -> p j t", j=2)
                    dst = PJ[:, :, 4 * i + half:4 * i + half + 3:2].rearrange("p t j -> p j t")
                    m = drain(b, full, ("act", "dve")[i], dst, src, free.get("PJ", []))
                pj.append(m)
                yield
            for i in range(2):
                half = NG // 2
                b, full = fill(lambda M: [tr(M[:, g * DH:(g + 1) * DH],
                                             PJ[:, (i * half + g) * TK:(i * half + g + 1) * TK, :].rearrange("d t e -> d (t e)"))
                                          for g in range(half)], pj)
                pr = drain(b, full, "act", PR[:, i * half:(i + 1) * half, :],
                           psM[b][:, :].rearrange("p (g d) -> p g d", d=DH), free.get("PR", []))
                yield
            free["PJ"] = [full]
            b, full = fill(lambda M: [tr(M[:, g * 2 * G2:(g + 1) * 2 * G2], GE[:, g * TK:(g + 1) * TK, :].rearrange("p t h -> p (t h)"))
                                      for g in range(NG)], [ge])
            free["GE"] = [full]
            m = drain(b, full, "act", GS[:, :, :, :].rearrange("p a b e -> p (a b e)"), psM[b][:, :], free.get("GS", []))
            chain = Background(choose(p, m), "choose", clock[0], clock[0] + 6)
            stages.append(chain)
            yield
            for i in range(4):
                project("q", i)
                yield
                project("k", i)
                yield
            chain.finish()
            mt = made["MT", p]
            bt = made["BT", p]
            for c in range(NC):
                b, full = fill(lambda M: [mm(M[par * DH:(par + 1) * DH, k * P:(k + 1) * P], PR[:, c * QG + k, :],
                                             BT[:, c % 2, par, k, :]) for k in range(QG) for par in range(2)], [bt[c], pr])
                free["BT", c % 2] = [full]
                free["PR"] = [full]
                if c + 2 < NC:
                    bt.append(value_blocks(c + 2, mt))
                made["VT", c] = drain(b, full, ("act", "dve")[c % 2], VT[:, c * QG * TK:(c + 1) * QG * TK, :],
                                      psM[b][:, :].rearrange("p (t h) -> p t h", h=HP), free.get("VT", []))
                yield
            free["MT"] = [bt[-1]]
            for i in range(4):
                jt, hp0 = i // 2, 4 * (i % 2)
                b, full = fill(lambda M: [tr(M[:, j * P:(j + 1) * P], VT[:, jt * P:(jt + 1) * P, hp0 + j]) for j in range(4)],
                               [made["VT", a] for a in range(NC)])
                made["V", p, i] = drain(b, full, ("act", "dve")[i % 2], V[:, o, jt, hp0:hp0 + 4, :],
                                        psM[b][:, :].rearrange("p (j t) -> p j t", j=4), free.get(("V", o), []))
                yield
            free["VT"] = [full]

        def value_blocks(b, ready):
            shape = [P, QG, TK, HP]
            d4 = delta[:, :].rearrange("p (t h) -> p t h", h=HP).unsqueeze(1).to_broadcast(shape)
            for par in range(2):
                dst = BT[:, b % 2, par, :, :].rearrange("p k (t h) -> p k t h", h=HP)
                gates = MT[:, par, b, :].rearrange("p (k h) -> p k h", h=HP).unsqueeze(2).to_broadcast(shape)
                m = put("pool", lambda e, dst=dst, gates=gates: e.tensor_tensor(dst, gates, d4, ALU.mult),
                        [ready, const, *free.get(("BT", b % 2), [])], s_blk)
            return m

        def blocks(c, gates, ready):
            shape = [P, QG * 2, TK, E]
            dst = BLK[:, c, :, :].rearrange("p a (t e) -> p a t e", e=E)
            g4 = gates.unsqueeze(2).to_broadcast(shape)
            d4 = delta[:, :].rearrange("p (t e) -> p t e", e=E).unsqueeze(1).to_broadcast(shape)
            return put("pool", lambda e: e.tensor_tensor(dst, g4, d4, ALU.mult),
                       [ready, const, *free.get(("BLK", c), [])], s_blk)

        def epilogue(p, s, attention):
            o = p % 2
            blk = [blocks(c, MASK[:, o, c * QG * 2:(c + 1) * QG * 2, :], made["MASK", p]) for c in range(NC)]
            free["MASK", o] = [blk[-1]]
            an = [None] * NC
            for c in range(NC + 1):
                if c < NC:
                    b, full = fill(lambda M: [tr(M[:, j * P:(j + 1) * P],
                                                 AT[:, o, (c * QG + j) * TK:(c * QG + j + 1) * TK, :].rearrange("p t h -> p (t h)"))
                                              for j in range(QG)], [made["AT", p]])
                    an[c] = drain(b, full, ("act", "dve")[c % 2], AN[:, c % 2, :, :],
                                  psM[b][:, :].rearrange("p (j t) -> p j t", j=QG), free.get(("AN", c % 2), []))
                    if c == NC - 1:
                        free["AT", o] = [full]
                    yield
                if c > 0:
                    a = c - 1
                    b, full = fill(lambda M: [mm(M[par * DH:(par + 1) * DH, g * P:(g + 1) * P],
                                                 AN[:, a % 2, g, par * DH:(par + 1) * DH], BLK[:, a, 2 * g + par, :])
                                              for g in range(QG) for par in range(2)], [an[a], blk[a]])
                    free["AN", a % 2] = [full]
                    free["BLK", a] = [full]
                    n = QG * TK
                    made["OT", a] = drain(b, full, ("act", "dve")[a % 2],
                                          OT[:, :, a * n:(a + 1) * n].rearrange("p e t -> p t e"),
                                          psM[b][:, :].rearrange("p (t e) -> p t e", e=E), free.get("OT", []))
                    yield
            b, full = fill(lambda M: [mm(M[:, n * C:(n + 1) * C], OT[:, e, n * P:(n + 1) * P], wo[:, e, :], e == 0, e == E - 1)
                                      for n in range(NT) for e in range(E)], [made["OT", a] for a in range(NC)])
            free["OT"] = [full]
            xs = X[:, s % XRING, :, :].rearrange("p n c -> p (n c)")
            m = put("dve", lambda e, b=b: e.scalar_tensor_tensor(xs, psM[b][:, 0:NT * C], 0.5, xs, ALU.mult, ALU.add),
                    [full], s_free[b])
            bank_free[b] = [m]
            x_ready[s] = [m]
            yield
            if not attention:
                stored[s] = put("sp", lambda e: e.dma_start(out[s].rearrange("(n p) c -> p n c", p=P), X[:, s % XRING]),
                                [m], s_out, 16)
                return
            yield from layernorm(1, lambda n: X[:, s % XRING, n, :], lambda n: XN[:, 1, n, :], [m], free.get("XN1", []))
            yield
            b, full = transpose_tokens(1, lambda n: XN[:, 1, n, :], None)
            free["XN1"] = [full]
            xnt = drain(b, full, "act", XNT[:, 1, :], psM[b][:, 0:T], free.get("XNT1", []))
            yield
            for n in range(NT):
                b, full = fill(lambda M: [mm(M[:, :], XNT[:, 1, n * P:(n + 1) * P], awkv[:, :])], [xnt, resid])
                kv = put("dve", lambda e, b=b, n=n: e.tensor_tensor(KV[:, n, :], psM[b][:, :], bkv[:, :], ALU.add),
                         [full, *free.get("KV", [])], s_free[b])
                bank_free[b] = [kv]
                yield
            b, full = fill(lambda M: [mm(M[:, 0:T], awq[:, :], XNT[:, 1, :])], [xnt, resid])
            free["XNT1"] = [full]
            aq = put("dve", lambda e, b=b: e.tensor_scalar(AQ[:, :], psM[b][:, 0:T], bq[:, 0:1], None, ALU.add),
                     [full, *free.get("AQ", [])], s_free[b])
            bank_free[b] = [aq]
            yield
            b, full = fill(lambda M: [mm(M[:, k * C:(k + 1) * C], KV[:, n, k * C:(k + 1) * C], KV[:, n, (2 + k) * C:(3 + k) * C],
                                         n == 0, n == NT - 1) for k in range(2) for n in range(NT)], [kv])
            free["KV"] = [full]
            m = put("dve", lambda e, b=b: e.scalar_tensor_tensor(S0[:, :], psM[b][:, 0:C], SSCALE, headmask[:, :],
                                                                 ALU.mult, ALU.mult), [full], s_dve)
            m = put("dve", lambda e, b=b: e.tensor_tensor(ST[:, :], psM[b][:, C:2 * C], S0[:, :], ALU.mult),
                    [m, *free.get("ST", [])], s_free[b])
            bank_free[b] = [m]
            yield
            b, full = fill(lambda M: [mm(M[:, n * C:(n + 1) * C], AQ[:, n * P:(n + 1) * P], ST[:, :]) for n in range(NT)],
                           [aq, m])
            free["ST"] = free["AQ"] = [full]
            m = drain(b, full, "act", AO[:, :, :], psM[b][:, 0:NT * C].rearrange("p (n c) -> p n c", n=NT),
                      free.get("AO", []))
            yield
            yield from layernorm(2, lambda n: AO[:, n, :], lambda n: AON[:, n, :], [m], free.get("AON", []))
            free["AO"] = [normed[2]]
            yield
            b, full = transpose_tokens(2, lambda n: AON[:, n, :], None)
            free["AON"] = [full]
            m = put("dve", lambda e, b=b: e.tensor_scalar(AOT[:, :], psM[b][:, 0:T], lng[:, 0:1], lnb[:, 0:1], ALU.mult, ALU.add),
                    [full, *free.get("AOT", [])], s_free[b])
            bank_free[b] = [m]
            yield
            b, full = fill(lambda M: [mm(M[:, n * C:(n + 1) * C], AOT[:, n * P:(n + 1) * P], awo[:, :]) for n in range(NT)], [m])
            free["AOT"] = [full]
            m = put("dve", lambda e, b=b: e.tensor_tensor(xs, psM[b][:, 0:NT * C], xs, ALU.add), [full], s_free[b])
            bank_free[b] = [m]
            xn = X[:, s % XRING, :, :]
            m = put("pool", lambda e: e.tensor_tensor(xn, xn, bo[:, :].unsqueeze(1).to_broadcast([P, NT, C]), ALU.add),
                    [m], s_pool)
            x_ready[s] = [m]

        score_free = [[], []]
        pt_free = [[], []]
        o_free = []
        pb_free = [[], [], []]
        ptb_free = [[] for _ in range(4)]
        maxed, normed_head, copied = {}, {}, {}

        exped = {}

        def scores(n):
            p, h = divmod(n, H)
            o, hp, par, r = p % 2, h // 2, h % 2, n % 3
            lo = par * DH
            for it in range(NT):
                m = put("pe", mm(psS[n % 2][:, it, :], QT[lo:lo + DH, o, hp, it * P:(it + 1) * P], KT[lo:lo + DH, o, hp, :]),
                        [made["q", p, hp // 2], made["k", p, hp // 2], *score_free[n % 2]] if it == 0 else (),
                        s_score if it == NT - 1 else None)
            if h == H - 1:
                free["QK", o] = [m]
            maxed[n] = put("dve", lambda e: e.tensor_reduce(NMAX[:, r, :], psS[n % 2][:, :, :], AX_X, ALU.max, negate=True),
                           [m], s_max)

        def exponentials(n):
            r = n % 3
            for it in range(NT):
                m = put("act", lambda e, it=it: e.activation(PB[:, r, it, :], psS[n % 2][:, it, :], ACT.Exp,
                                                            bias=NMAX[:, r, it:it + 1], accum_out=SUM[:, r, it:it + 1]),
                        [maxed[n], *pb_free[r]], s_exp)
            score_free[n % 2] = exped[n] = [m]

        def normalise(n):
            r = n % 3
            m = put("dve", lambda e: e.reciprocal(RSUM[:, r, :], SUM[:, r, :]), exped[n], s_rsum)
            for it in range(NT):
                m2 = put("dve", lambda e, it=it: e.tensor_scalar(PB[:, r, it, :], PB[:, r, it, :], RSUM[:, r, it:it + 1],
                                                                 None, ALU.mult), [m], s_norm)
            normed_head[n] = m2

        def turn(n):
            r = n % 3
            steps = [tr(psT[n % 2][:, jt, it * P:(it + 1) * P], PB[:, r, it, jt * P:(jt + 1) * P])
                     for it in range(NT) for jt in range(NT)]
            for k, step in enumerate(steps):
                m = put("pe", step, [normed_head[n], *pt_free[n % 2]] if k == 0 else (), s_pt if k == 3 else None)
            pb_free[r] = [m]
            m = copy("act", PT[:, n % 4, :, :], psT[n % 2][:, :, :], [m, *ptb_free[n % 4]], s_ptc)
            pt_free[n % 2] = [m]
            copied[n] = m

        def product(n):
            p, h = divmod(n, H)
            o, hp = p % 2, h // 2
            vs = [made["V", p, 2 * jt + hp // 4] for jt in range(NT)]
            for jt in range(NT):
                for par in range(2):
                    first = jt == par == 0
                    last = jt == NT - 1 and par == 1
                    m = put("pe", mm(psO[par * DH:(par + 1) * DH, :], V[:, o, jt, hp, par * DH:(par + 1) * DH],
                                     PT[:, (n + par) % 4, jt, :], jt == 0, jt == NT - 1),
                            [copied[n], copied[n + 1], *vs, *o_free] if first else (), s_pv if last else None)
            ptb_free[n % 4] = ptb_free[(n + 1) % 4] = [m]
            if h == H - 2:
                free["V", o] = [m]
            m = put("act", lambda e: e.activation(AT[:, o, :, hp], psO[:, :], ACT.Copy), [m, *free.get(("AT", o), [])], s_oc)
            o_free[:] = [m]
            made["AT", p] = m

        LEAD = 4
        order = [(s, True) for s in range(min(LEAD, NSEQ))]
        for s in range(NSEQ):
            order.append((s, False))
            if s + LEAD < NSEQ:
                order.append((s + LEAD, True))
        if NSEQ < LEAD:
            raise ValueError("too few sequences")

        for first in (norm(0, order[0][0]), prologue(0, order[0][0]), norm(1, order[1][0])):
            for _ in first:
                pass
        total = len(order) * H
        scores(0)
        exponentials(0)
        for n in range(total + 4):
            clock[0] = n
            p, h = divmod(n, H)
            if h == 0 and p + 1 < len(order):
                stages.append(Background(prologue(p + 1, order[p + 1][0]), "prologue", n, n + H - 0.75))
            if h == H - 4 and p + 2 < len(order):
                stages.append(Background(norm(p + 2, order[p + 2][0]), "norm", n, n + 3))
            if h == 2 and 0 < p <= len(order):
                stages.append(Background(epilogue(p - 1, *order[p - 1]), order[p - 1][1], n, n + H - 2.75))

            def background(now):
                while any([w.due(now) for w in stages]):
                    for w in list(stages):
                        if w.due(now):
                            w.step()

            if n + 1 < total:
                if (n + 1) % H == 0:
                    for w in stages:
                        w.finish()
                    stages.clear()
                scores(n + 1)
            background(n + 0.25)
            if n < total:
                normalise(n)
            background(n + 0.5)
            if n + 1 < total:
                exponentials(n + 1)
            if 1 <= n <= total:
                turn(n - 1)
            background(n + 0.75)
            if n >= 3 and (n - 3) % 2 == 0 and n - 3 < total:
                product(n - 3)
            background(n + 1)
        for w in stages:
            w.finish()
        queue["sp"].append(("wait", s_out, count[s_out]))

        block = ctx.enter_context(nc.Block())

        @block.sync
        def _(eng):
            play("sp", eng)

        @block.tensor
        def _(eng):
            play("pe", eng)

        @block.vector
        def _(eng):
            play("dve", eng)

        @block.scalar
        def _(eng):
            play("act", eng)

        @block.gpsimd
        def _(eng):
            play("pool", eng)


def kernel(**inputs):
    import numpy as np
    import concourse.bacc as bacc
    from concourse.bass_utils import run_bass_kernel_spmd

    a = {k: np.asarray(v) for k, v in inputs.items()}
    x = a["L0_attn_x"]
    n, t, c = x.shape
    h, dh = a["L0_ffn_Wq"].shape[:2]
    e = a["L0_ffn_Wv"].shape[0]
    head = 8
    one = np.float32(1)
    row, col = np.arange(P)[:, None], np.arange(P)[None, :]
    arrays = {
        "x": x,
        "WqT": a["L0_ffn_Wq"].reshape(h * dh, c).T,
        "WkT": a["L0_ffn_Wk"].reshape(h * dh, c).T,
        "WvT": a["L0_ffn_Wv"].reshape(e * dh, c).T,
        "WgT": np.concatenate([a["L0_ffn_Ws"], a["L0_ffn_Wd"]], axis=1).reshape(h * 2 * e, c).T,
        "WoT": a["L0_ffn_Wo"].transpose(2, 0, 1),
        "aWq": a["L0_attn_Wq"],
        "aWkv": np.concatenate([*a["L0_attn_Wk"], *a["L0_attn_Wv"]], axis=1),
        "aWo": a["L0_attn_Wo"],
        "b_q": a["L0_attn_bq"],
        "b_kv": np.concatenate([*a["L0_attn_bk"], *a["L0_attn_bv"]]),
        "b_o": a["L0_attn_bo"],
        "ln_g": a["L0_attn_ln_g"],
        "ln_b": a["L0_attn_ln_b"],
        "ident": np.where(row == col, one, 0 * one),
        "order": (lambda r: np.where(((r // 64) * 64 + (r % 4) * 16 + (r // 4 % 4) * 4 + r // 16 % 4) == col, one, 0 * one))(row),
        "delta": np.where(row // 8 == col // 8, one, 0 * one),
        "ramp": np.broadcast_to(np.arange(e, 0, -1, dtype=np.float32), (P, e)),
        "heads": np.where(row // head == col // head, one, 0 * one),
    }
    arrays = {k: np.ascontiguousarray(v) for k, v in arrays.items()}
    nc = bacc.Bacc("TRN2", target_bir_lowering=False, num_devices=1)
    args = [nc.dram_tensor(f"in_{k}", v.shape, mybir.dt.from_np(v.dtype), kind="ExternalInput").ap()
            for k, v in arrays.items()]
    out = nc.dram_tensor("out", x.shape, F32, kind="ExternalOutput").ap()
    macaron_kernel(nc, *args, out)
    r = run_bass_kernel_spmd(nc, [{f"in_{k}": v for k, v in arrays.items()}], core_ids=[0])
    return r.results[0]["out"]
```

```python
from contextlib import ExitStack

import concourse.bass as bass
from concourse import mybir

F32 = mybir.dt.float32
F32R = mybir.dt.float32r
ALU = mybir.AluOpType
ACT = mybir.ActivationFunctionType
AX_X = mybir.AxisListType.X

P = 128
TK = 16
EPS = 1e-5
MISC = 3
XRING = 8
LOWEST = -3.0e38
SPANS = {"prologue": (0, 4.4), "choose": (4, 9.1), "values": (12, 15.75), "attend": (2, 5.9), "norm": (13, 15), "epilogue": (3, 12.5)}
TURN = "SCTEP"
COPIES = {"XNT": "a", "XKT": "v", "GE": "a", "PJ": "av", "PR": "aa", "GS": "a", "VT": "avav", "V": "avav", "AN": "avav",
          "OT": "avav", "AX": "a", "AO": "a", "PT": "aaaa", "AT": "a"}
LIGHT = 0.206
LEAD = 4
PLEAD = 6
HANDOVER = 350
DMA_NS = 2000
SMALL = {"pe": 108.90000000000002, "act": 32.0, "dve": 59.400000000000006, "pool": 340.3125, "sp": 60}
PER_ELEMENT = {"act": 0.6664680000000002, "dve": 0.7560000000000001, "pool": 2.3}
BIAS = {"act": 0, "dve": 0}
SLACK = -200
EAGER = 150
TLAG = 1


def macaron_kernel(nc, x, WqT, WkT, WvT, WgT, WoT, aWq, aWkv, aWo, b_q, b_kv, b_o, ln_g, ln_b,
                   ident_d, order_d, delta_d, token_d, group_d, ramp_d, heads_d, out):
    NSEQ, T, C = x.shape
    NT = T // P
    E, DH = WoT.shape[1], WoT.shape[0]
    H = WqT.shape[1] // DH
    HP = H // 2
    NG = T // TK
    NP = 2 * NG
    G2 = 2 * E
    HR = P // G2
    R = H // HR
    QG = 4
    NC = NG // QG
    CH = 2
    NCH = HP // CH
    QRING = 3
    QSCALE = float(DH) ** -0.5
    SSCALE = (1.0 / 512.0) ** 2
    assert C == P and 2 * DH == P and TK * HP == P and TK * E == P and T == 2 * P and H == 16

    ctx = ExitStack()
    with ctx:
        def sb(name, shape, dtype=F32):
            return ctx.enter_context(nc.sbuf_tensor(name, shape, dtype))

        def pb(name, shape):
            return ctx.enter_context(nc.psum_tensor(name, shape, F32))

        ident = sb("ident", [P, P])
        keyorder = sb("keyorder", [P, P])
        delta = sb("delta", [P, TK * E])
        token = sb("token", [P, P])
        group = sb("group", [P, P // TK])
        ramp = sb("ramp", [P, E])
        headmask = sb("headmask", [P, P])
        wq = sb("wq", [P, 2, H * DH], F32R)
        wk = sb("wk", [P, 2, H * DH], F32R)
        wv = sb("wv", [P, 2, E * DH], F32R)
        wg = sb("wg", [P, H * G2])
        wo = sb("wo", [P, E, C])
        awq = sb("awq", [P, C])
        awkv = sb("awkv", [P, 4 * C])
        awo = sb("awo", [P, C])
        bq = sb("bq", [P, 1])
        bkv = sb("bkv", [P, 4 * C])
        bo = sb("bo", [P, C])
        lng = sb("lng", [P, 1])
        lnb = sb("lnb", [P, 1])
        X = sb("X", [P, XRING, NT, C])
        XN = sb("XN", [P, 2, NT, C])
        XNT = sb("XNT", [P, 2, T])
        XQ = sb("XQ", [P, 2, 2, T], F32R)
        XK = sb("XK", [P, 2, 2, T], F32R)
        STAT = sb("STAT", [P, 3, NT, 6])
        MV = sb("MV", [P, 3, NT, 2])
        RSTD = sb("RSTD", [P, 3, NT])
        power = sb("power", [P, NT])
        LO = sb("LO", [P, 2, CH, T], F32R)
        QS = sb("QS", [P, QRING, CH, 2, T], F32R)
        KS = sb("KS", [P, QRING, CH, 2, T], F32R)
        KL = sb("KL", [P, QRING, CH, T], F32R)
        GS = sb("GS", [P, NP, 2, E])
        F1 = sb("F1", [P, NP, 2, E])
        FW = sb("FW", [P, NP, 2, E])
        GM = sb("GM", [P, NP, 2, E])
        MAXV = sb("MAXV", [P, NP * 2])
        MAXR = sb("MAXR", [P, NP * 2])
        SG = sb("SG", [P, NP, E])
        MIX = sb("MIX", [P, 2, NG, E])
        MASK = sb("MASK", [P, 3, NP, E])
        PJ_GE = sb("PJ_GE", [DH + 2 * G2, T, E])
        PJ = PJ_GE[0:DH, :, :]
        GE = PJ_GE[DH:DH + 2 * G2, :, :]
        PR = sb("PR", [P, NG, DH])
        BLK = sb("BLK", [P, 2, QG * 2, TK * E])
        MT = sb("MT", [P, 2, NC, QG * HP])
        BT = sb("BT", [P, 2, 2, QG, P])
        VT = sb("VT", [P, T, HP])
        V = sb("V", [P, 2, NT, HP, P])
        PB = sb("PB", [P, 3, NT, T])
        PT = sb("PT", [P, 4, NT, T])
        NMAX = sb("NMAX", [P, 4, NT])
        SUM = sb("SUM", [P, 2, NT, 2, HP])
        SUMT = sb("SUMT", [P, NT, 2, P])
        RSUM = sb("RSUM", [P, NG, 2])
        AT = sb("AT", [P, 2, T, HP])
        AN = sb("AN", [P, 2, QG, P])
        OT = sb("OT", [P, E, T])
        KV = sb("KV", [P, NT, 4 * C])
        S0 = sb("S0", [P, C])
        ST = sb("ST", [P, C])
        AQ = sb("AQ", [P, T])
        AO = sb("AO", [P, NT, C])
        AON = sb("AON", [P, NT, C])
        AOT = sb("AOT", [P, T])

        psS = [pb(f"psS{i}", [P, NT, T]) for i in range(2)]
        psT = [pb(f"psT{i}", [P, NT, T]) for i in range(2)]
        psO = pb("psO", [P, T])
        psM = [pb(f"psM{i}", [P, 512]) for i in range(MISC)]

        count, handle = {}, {}

        def sem(name):
            handle[name] = ctx.enter_context(nc.semaphore(name))
            count[name] = 0
            return name

        s_const = sem("s_const")
        s_x = [sem(f"s_x{i}") for i in range(XRING)]
        s_move = [sem(f"s_move{i}") for i in range(4)]
        s_hi = sem("s_hi")
        s_out = sem("s_out")
        s_dve = sem("s_dve")
        s_act = sem("s_act")
        s_pool = sem("s_pool")
        s_blk = sem("s_blk")
        s_score = sem("s_score")
        s_max = sem("s_max")
        s_exp = sem("s_exp")
        s_pt = sem("s_pt")
        s_ptc = [sem(f"s_ptc{i}") for i in range(2)]
        s_pv = sem("s_pv")
        s_oc = sem("s_oc")
        s_fill = [sem(f"s_fill{i}") for i in range(MISC)]
        s_free = [sem(f"s_free{i}") for i in range(MISC)]

        queue = {"pe": [], "dve": [], "act": [], "pool": [], "sp": []}
        waited = {}
        clock = dict.fromkeys(queue, 0.0)
        reached = {}

        def ready_at(marks):
            return max([reached[m] for m in marks], default=0.0)

        def put(engine, step, waits=(), signal=None, by=1, ns=None):
            start = max(clock[engine], ready_at(waits) + (HANDOVER if waits else 0))
            clock[engine] = start + (ns or SMALL[engine])
            for name, value in waits:
                if value > waited.get((engine, name), 0):
                    waited[engine, name] = value
                    queue[engine].append(("wait", name, value))
            queue[engine].append(("do", step, signal, by))
            if signal is not None:
                count[signal] += by
                reached[signal, count[signal]] = clock[engine] + (DMA_NS if engine == "sp" else 0)
                return signal, count[signal]

        def play(engine, eng):
            for what in queue[engine]:
                if what[0] == "wait":
                    eng.wait_ge(handle[what[1]], what[2])
                else:
                    ins = what[1](eng)
                    if what[2] is not None:
                        ins.then_inc(handle[what[2]], what[3])

        def per_element(engine, elements):
            return SMALL[engine] + elements * PER_ELEMENT[engine]

        def copy(engine, dst, src, waits, signal, scale=None):
            size = dst.free_size()
            if engine is None:
                engine = min(("act", "dve"), key=lambda e: max(clock[e], ready_at(waits)) + per_element(e, size) + BIAS[e])
            ns = per_element(engine, size)
            if engine == "act":
                return put("act", lambda e: e.activation(dst, src, ACT.Copy, scale=scale or 1.0),
                           waits, signal, ns=ns)
            if scale is None:
                return put("dve", lambda e: e.tensor_copy(dst, src), waits, signal, ns=ns)
            return put("dve", lambda e: e.tensor_scalar(dst, src, scale, None, ALU.mult), waits, signal, ns=ns)

        bank_at = [0]
        bank_free = [[] for _ in range(MISC)]

        def fill(steps, waits):
            b = bank_at[0] % MISC
            bank_at[0] += 1
            before = load[0]
            todo = steps(psM[b])
            for n, step in enumerate(todo):
                last = n == len(todo) - 1
                full = put("pe", step, list(waits) + bank_free[b] if n == 0 else (),
                           s_fill[b] if last else None, ns=(load[0] - before) * 1000 / len(todo))
            return b, full

        def drain(b, full, engine, dst, src, waits=(), scale=None):
            m = copy(engine, dst, src, [full, *waits], s_free[b], scale)
            bank_free[b] = [m]
            return m

        load = [0.0]

        def mm(dst, lhsT, rhs, start=True, stop=True):
            columns = max(64, rhs.free_size()) * (1 if lhsT.free_size() > DH else 0.5)
            load[0] += 4 * columns / 2400
            return lambda e: e.matmul(dst, lhsT, rhs, start=start, stop=stop)

        def split_mm(dst, w, i, x2):
            columns = slice(i * P, (i + 1) * P)
            terms = ((0, 0), (0, 1), (1, 0))
            load[0] += 3 * T / 2400
            return [lambda e, a=a, c=c, n=n: e.matmul(dst, w[:, a, columns], x2[:, c, :], start=n == 0, stop=n == 2)
                    for n, (a, c) in enumerate(terms)]

        def tr(dst, src, first=0):
            rows = slice(first, first + src.shape[0])
            load[0] += 2 * P / 2400
            return lambda e: e.transpose(dst, src, ident[rows, rows])

        raw_q = VT[:, 0:P, :].rearrange("p t h -> p (t h)")
        raw_k = VT[:, P:T, :].rearrange("p t h -> p (t h)")
        raw_v = V[:, 1, 0, 0:4, :].rearrange("p h d -> p (h d)")
        consts = [(ident, ident_d), (keyorder, order_d), (delta, delta_d), (token, token_d), (group, group_d), (ramp, ramp_d), (headmask, heads_d), (raw_q, WqT),
                  (wg, WgT), (raw_k, WkT), (raw_v, WvT), (awq, aWq), (awkv, aWkv), (awo, aWo)]
        loaded_x = {}
        stored = {}

        def load_x(s):
            waits = [stored[s - XRING]] if s >= XRING else []
            loaded_x[s] = put("sp", lambda e: e.dma_start(X[:, s % XRING], x[s].rearrange("(n p) c -> p n c", p=P)),
                              waits, s_x[s % XRING], 16)

        load_x(0)
        for dst, src in consts:
            put("sp", lambda e, d=dst, s=src: e.dma_start(d[:], s), (), s_const, 16)
        for half in range(2):
            put("sp", lambda e, h=half: e.dma_start(wo[h * DH:(h + 1) * DH], WoT), (), s_const, 16)
        for dst, src in ((bq, b_q), (lng, ln_g), (lnb, ln_b)):
            put("sp", lambda e, d=dst, s=src: e.dma_start(d[:, :], s.rearrange("(p a) -> p a", a=1)), (), s_const, 16)
        for dst, src in ((bkv, b_kv), (bo, b_o)):
            put("sp", lambda e, d=dst, s=src: e.dma_start(d[:, :], s.partition_broadcast(P)), (), s_const, 16)
        const = (s_const, count[s_const])
        put("dve", lambda e: e.tensor_tensor(awq[:, :], awq[:, :], ident[:, :], ALU.add), [const], s_dve)
        for i in range(4):
            resid = put("dve", lambda e, i=i: e.tensor_tensor(awkv[:, i * C:(i + 1) * C], awkv[:, i * C:(i + 1) * C],
                                                              ident[:, :], ALU.add), [], s_dve)

        for raw, w in ((raw_q, wq), (raw_k, wk), (raw_v, wv)):
            m = put("act", lambda e, raw=raw, w=w: e.activation(w[:, 0, :], raw, ACT.Copy), [const], s_hi, ns=900)
            split = put("dve", lambda e, raw=raw, w=w: e.tensor_tensor(w[:, 1, :], raw, w[:, 0, :].bitcast(F32), ALU.subtract),
                        [m], s_dve, ns=1100)

        powers = put("pool", lambda e: e.memset(power[:, :], -0.5), (), s_pool)

        def layernorm(k, src, dst, ready, dst_free):
            for n in range(NT):
                m = put("dve", lambda e, n=n: e.bn_stats(STAT[:, k, n, :], src(n)), ready, s_dve)
            for n in range(NT):
                m = put("dve", lambda e, n=n: e.bn_aggr(MV[:, k, n, :], STAT[:, k, n, :]), [m], s_dve)
            yield [m]
            m = put("pool", lambda e: e.tensor_scalar(RSTD[:, k, :], MV[:, k, :, 1], EPS, None, ALU.add), [m], s_pool)
            m = put("pool", lambda e: e.tensor_tensor(RSTD[:, k, :], RSTD[:, k, :], power[:, :], ALU.pow), [m, powers], s_pool)
            yield [m]
            for n in range(NT):
                m2 = put("dve", lambda e, n=n: e.tensor_scalar(dst(n), src(n), MV[:, k, n, 0:1], RSTD[:, k, n:n + 1],
                                                               ALU.subtract, ALU.mult), [m, *dst_free], s_dve)
            normed[k] = m2

        normed = {}
        x_ready = {}
        free = {"VT": [split], ("V", 1): [split]}
        made = {}

        def transpose_tokens(k, src, dst):
            b, full = fill(lambda M: [tr(M[:, n * P:(n + 1) * P], src(n)) for n in range(NT)], [normed[k], const])
            return b, full

        stages = []

        sizes = {}

        class Background:

            def __init__(self, steps, kind, start, end):
                self.steps, self.kind, self.start, self.end = steps, kind, start, end
                self.size, self.at, self.done = sizes.get(kind, 20.0), 0.0, False
                self.waits = []

            def step(self):
                before = load[0]
                self.waits = next(self.steps, "end")
                ended, self.waits = self.waits == "end", self.waits or []
                if ended:
                    self.done = True
                    sizes[self.kind] = self.at
                self.at += load[0] - before + LIGHT

            def due(self, now):
                goal = self.size * (now - self.start) / (self.end - self.start)
                return not self.done and self.at < goal

            def ready(self):
                return max(ready_at(self.waits), ready_at(bank_free[bank_at[0] % MISC]))

            def finish(self):
                while not self.done:
                    self.step()

        def choose(p):
            m = made["GS", p]
            gall, f1, fw, gm = ([t[:, :, :, :].rearrange("p a b e -> p (a b) e") for t in (GS, F1, FW, GM)])
            shape = [P, 2 * NP, E]

            def over_e(t):
                return t[:, :].unsqueeze(2).to_broadcast(shape)

            ramps = ramp[:, :].unsqueeze(1).to_broadcast(shape)
            sig = put("act", lambda e: e.activation(SG[:, :, :], GS[:, :, 0, :], ACT.Exp, scale=-1.0),
                      [m, *free.get("SG", [])], s_act, ns=260)
            yield [m]

            def pick(values, m, chosen):
                m = put("dve", lambda e: e.tensor_reduce(MAXV[:, :], values, AX_X, ALU.max), [m], s_dve, ns=600)
                yield
                m = put("dve", lambda e: e.tensor_tensor(fw, values, over_e(MAXV), ALU.is_equal), [m], s_dve, ns=600)
                yield
                m = put("dve", lambda e: e.tensor_tensor(fw, fw, ramps, ALU.mult), [m], s_dve, ns=600)
                yield
                m = put("dve", lambda e: e.tensor_reduce(MAXR[:, :], fw, AX_X, ALU.max), [m], s_dve, ns=600)
                yield
                m = put("dve", lambda e: e.tensor_tensor(chosen, fw, over_e(MAXR), ALU.is_equal), [m], s_dve, ns=600)
                made["pick"] = m
                yield

            yield from pick(gall, m, f1)
            m = put("dve", lambda e: e.scalar_tensor_tensor(gm, f1, LOWEST, gall, ALU.mult, ALU.add),
                    [made["pick"]], s_dve, ns=600)
            yield from pick(gm, m, gm)
            m = made["pick"]
            put("dve", lambda e: e.tensor_tensor(MASK[:, p % 3, :, :], F1[:, :, 1, :], GM[:, :, 1, :], ALU.add),
                [m, *free.get(("MASK", p % 3), [])], s_dve)
            made["MASK", p] = (s_dve, count[s_dve])
            m = put("dve", lambda e: e.tensor_tensor(F1[:, :, 0, :], F1[:, :, 0, :], GM[:, :, 0, :], ALU.add), [m], s_dve)
            yield
            m2 = put("dve", lambda e: e.tensor_scalar(SG[:, :, :], SG[:, :, :], 1.0, None, ALU.add), [sig], s_dve, ns=300)
            m2 = put("dve", lambda e: e.reciprocal(SG[:, :, :], SG[:, :, :]), [m2, m], s_dve, ns=1700)
            yield
            m = put("dve", lambda e: e.tensor_tensor(MIX[:, :, :, :].rearrange("p a g e -> p g a e"),
                                                     F1[:, :, 0, :].rearrange("p (g a) e -> p g a e", a=2),
                                                     SG[:, :, :].rearrange("p (g a) e -> p g a e", a=2), ALU.mult),
                    [m2], s_dve)
            free["SG"] = [m]
            free["GS"] = [m]
            yield
            mt = put("dve", lambda e: e.transpose(MT[:, :, :, :].rearrange("p a b c -> p (a b c)"),
                                                  MIX[:, :, :, :].rearrange("p a g e -> p (a g e)")),
                     [m, *free.get("MT", [])], s_dve, ns=330)
            made["MT", p] = mt
            yield
            made["BT", p] = [value_blocks(c, mt) for c in range(2)]

        def norm(p, s):
            if s not in loaded_x:
                load_x(s)
            ready = x_ready.get(s, [loaded_x[s]])
            yield from layernorm(0, lambda n: X[:, s % XRING, n, :], lambda n: XN[:, 0, n, :], ready, free.get("XN0", []))

        def project(c, k):
            p, i = divmod(c, NCH)
            o, ring = p % 2, c % QRING
            w, xt, stack = ((wq, XQ, QS), (wk, XK, KS))[k]
            both, lo = stack[:, ring, :, :, :], (LO[:, c % 2, :, :], KL[:, ring, :, :])[k]
            scale = (QSCALE, 1.0)[k]
            stack_free = free.get(("QK", ring), [])
            b, full = fill(lambda M: [step for j in range(CH)
                                      for step in split_mm(M[:, j * T:(j + 1) * T], w, CH * i + j, xt[:, o, :, :])], [*made["XT", p], split])
            free["XQ" if k == 0 else "XK", o] = [full]
            src = psM[b][:, :].rearrange("p (j t) -> p j t", j=CH)
            m = put("act", lambda e: e.activation(both, src.unsqueeze(2).to_broadcast([P, CH, 2, T]), ACT.Copy, scale=scale),
                    [full, *stack_free], s_hi, ns=900)
            low = put("dve", lambda e: e.scalar_tensor_tensor(lo, src, scale, both[:, :, 0, :].bitcast(F32), ALU.mult, ALU.subtract),
                      [m, *(stack_free if k else free.get(("LO", c % 2), []))], s_free[b], ns=600)
            bank_free[b] = [low]
            for par in range(2):
                own, other = slice(par * DH, par * DH + DH), slice(DH - par * DH, 2 * DH - par * DH)
                moved = (LO[own, c % 2, :, :], both[own, :, par, :])[k]
                dma = put("sp", lambda e, par=par, other=other, moved=moved:
                          e.dma_start(both[other, :, par, :].bitcast(F32), moved.bitcast(F32)),
                          [low], s_move[2 * k + c % 2], 16)
            if k == 0:
                free["LO", c % 2] = [dma]
            made["QK"[k], c] = [low, dma]

        def prologue(p):
            o = p % 2
            b, full = transpose_tokens(0, lambda n: XN[:, 0, n, :], None)
            free["XN0"] = [full]
            xnt = drain(b, full, None, XNT[:, 0, :], psM[b][:, 0:T], free.get("XNT0", []))
            hi = put("act", lambda e: e.activation(XQ[:, o, 0, :], XNT[:, 0, :], ACT.Copy), [xnt, *free.get(("XQ", o), [])], s_hi, ns=260)
            xq = put("dve", lambda e: e.tensor_tensor(XQ[:, o, 1, :], XNT[:, 0, :], XQ[:, o, 0, :].bitcast(F32), ALU.subtract),
                     [hi], s_dve, ns=320)
            b, full = fill(lambda M: [(lambda e, n=n: e.transpose(M[:, n * P:(n + 1) * P], XN[:, 0, n, :], keyorder[:, :]))
                                      for n in range(NT)], [normed[0], const])
            free["XN0"] = [full]
            hi = put("act", lambda e, b=b: e.activation(XK[:, o, 0, :], psM[b][:, 0:T], ACT.Copy), [full, *free.get(("XK", o), [])], s_hi, ns=260)
            xkt = put("dve", lambda e, b=b: e.tensor_tensor(XK[:, o, 1, :], psM[b][:, 0:T], XK[:, o, 0, :].bitcast(F32), ALU.subtract),
                      [hi], s_free[b], ns=320)
            bank_free[b] = [xkt]
            made["XT", p] = [xq, xkt]
            yield [xnt]
            b, full = fill(lambda M: [mm(M[:, r * T:(r + 1) * T], wg[:, r * P:(r + 1) * P], XNT[:, 0, :])
                                      for r in range(R)], [xnt])
            free["XNT0"] = [full, xq]
            for q in range(HR // 2):
                ge = drain(b, full, None, GE[:, :, q::HR // 2].rearrange("p t r -> p r t"),
                           psM[b][q * 2 * G2:(q + 1) * 2 * G2, :].rearrange("p (r t) -> p r t", r=R), free.get("GE", []))
            yield [xkt]

            pj = []
            for i in range(2):
                b, full = fill(lambda M: [step for j in range(2)
                                          for step in split_mm(M[:, j * T:(j + 1) * T], wv, 2 * i + j, XK[:, o, :, :])], [xkt, split])
                for half in range(2):
                    src = psM[b][half * DH:(half + 1) * DH, :].rearrange("p (j t) -> p j t", j=2)
                    dst = PJ[:, :, 4 * i + half:4 * i + half + 3:2].rearrange("p t j -> p j t")
                    m = drain(b, full, None, dst, src, free.get("PJ", []))
                pj.append(m)
                yield pj if i else [xkt]
            pr = []
            for i in range(2):
                half = NG // 2
                b, full = fill(lambda M: [tr(M[:, g * DH:(g + 1) * DH],
                                             PJ[:, (i * half + g) * TK:(i * half + g + 1) * TK, :].rearrange("d t e -> d (t e)"))
                                          for g in range(half)], pj)
                pr.append(drain(b, full, None, PR[:, i * half:(i + 1) * half, :],
                           psM[b][:, :].rearrange("p (g d) -> p g d", d=DH), free.get("PR", [])))
                yield [ge] if i else [full]
            free["PJ"] = [full]
            made["PR", p] = pr
            b, full = fill(lambda M: [tr(M[:, g * 2 * G2:(g + 1) * 2 * G2], GE[:, g * TK:(g + 1) * TK, :].rearrange("p t h -> p (t h)"), DH)
                                      for g in range(NG)], [ge])
            free["GE"] = [full]
            m = drain(b, full, None, GS[:, :, :, :].rearrange("p a b e -> p (a b e)"), psM[b][:, :], free.get("GS", []))
            made["GS", p] = m

        def values(p):
            o, pr = p % 2, made["PR", p]
            mt = made["MT", p]
            bt = made["BT", p]
            for c in range(NC):
                b, full = fill(lambda M: [mm(M[par * DH:(par + 1) * DH, k * P:(k + 1) * P], PR[:, c * QG + k, :],
                                             BT[:, c % 2, par, k, :]) for k in range(QG) for par in range(2)], [bt[c], *pr])
                free["BT", c % 2] = [full]
                free["PR"] = [full]
                if c + 2 < NC:
                    bt.append(value_blocks(c + 2, mt))
                made["VT", c] = drain(b, full, None, VT[:, c * QG * TK:(c + 1) * QG * TK, :],
                                      psM[b][:, :].rearrange("p (t h) -> p t h", h=HP), free.get("VT", []))
                yield [bt[c + 1]] if c + 1 < NC else [made["VT", a] for a in range(NC)]
            free["MT"] = [bt[-1]]
            for i in range(4):
                jt, hp0 = i // 2, 4 * (i % 2)
                b, full = fill(lambda M: [tr(M[:, j * P:(j + 1) * P], VT[:, jt * P:(jt + 1) * P, hp0 + j]) for j in range(4)],
                               [made["VT", a] for a in range(NC)])
                made["V", p, i] = drain(b, full, None, V[:, o, jt, hp0:hp0 + 4, :],
                                        psM[b][:, :].rearrange("p (j t) -> p j t", j=4), free.get(("V", o), []))
                yield
            free["VT"] = [full]

        def value_blocks(b, ready):
            shape = [P, QG, TK, HP]
            d4 = delta[:, :].rearrange("p (t h) -> p t h", h=HP).unsqueeze(1).to_broadcast(shape)
            for par in range(2):
                dst = BT[:, b % 2, par, :, :].rearrange("p k (t h) -> p k t h", h=HP)
                gates = MT[:, par, b, :].rearrange("p (k h) -> p k h", h=HP).unsqueeze(2).to_broadcast(shape)
                m = put("pool", lambda e, dst=dst, gates=gates: e.tensor_tensor(dst, gates, d4, ALU.mult),
                        [ready, const, *free.get(("BT", b % 2), [])], s_blk, ns=1220)
            return m

        def blocks(c, gates, ready):
            shape = [P, QG * 2, TK, E]
            dst = BLK[:, c % 2, :, :].rearrange("p a (t e) -> p a t e", e=E)
            g4 = gates.unsqueeze(2).to_broadcast(shape)
            d4 = delta[:, :].rearrange("p (t e) -> p t e", e=E).unsqueeze(1).to_broadcast(shape)
            return put("pool", lambda e: e.tensor_tensor(dst, g4, d4, ALU.mult),
                       [ready, const, *free.get(("BLK", c % 2), [])], s_blk, ns=2300)

        def epilogue(p, s, attention):
            o = p % 2
            def mask_blocks(c):
                return blocks(c, MASK[:, p % 3, c * QG * 2:(c + 1) * QG * 2, :], masked)

            sums = SUM[:, o, :, :, :].rearrange("p n a h -> p (n a) h").unsqueeze(2).to_broadcast([P, 2 * NT, TK, HP])
            tokens = token[:, :].rearrange("p (t h) -> p t h", h=HP).unsqueeze(1).to_broadcast([P, 2 * NT, TK, HP])
            m = put("dve", lambda e: e.tensor_tensor(SUMT[:, :, :, :].rearrange("p n a (t h) -> p (n a) t h", h=HP), sums, tokens, ALU.mult),
                    [made["SUM", p], const, *free.get("SUMT", [])], s_dve, ns=600)
            free["SUM", o] = [m]
            yield [m]
            b, full = fill(lambda M: [mm(M[:, n * NG + par:(n + 1) * NG:2], SUMT[:, n, par, :], group[:, :])
                                      for n in range(NT) for par in range(2)], [m])
            free["SUMT"] = [full]
            m = put("dve", lambda e, b=b: e.reciprocal(RSUM[:, :, :].rearrange("p g a -> p (g a)"), psM[b][:, 0:NP]), [full], s_free[b], ns=220)
            bank_free[b] = [m]
            mask = MASK[:, p % 3, :, :]
            masked = put("dve", lambda e: e.tensor_tensor(mask, mask, RSUM[:, :, :].rearrange("p g a -> p (g a)").unsqueeze(2)
                                                          .to_broadcast([P, NP, E]), ALU.mult), [m, made["MASK", p]], s_dve, ns=300)
            blk = [mask_blocks(c) for c in range(2)]
            yield [made["AT", p]]
            an = [None] * NC
            for c in range(NC + 1):
                if c < NC:
                    b, full = fill(lambda M: [tr(M[:, j * P:(j + 1) * P],
                                                 AT[:, o, (c * QG + j) * TK:(c * QG + j + 1) * TK, :].rearrange("p t h -> p (t h)"))
                                              for j in range(QG)], [made["AT", p]])
                    an[c] = drain(b, full, None, AN[:, c % 2, :, :],
                                  psM[b][:, :].rearrange("p (j t) -> p j t", j=QG), free.get(("AN", c % 2), []))
                    if c == NC - 1:
                        free["AT", o] = [full]
                    yield [an[c - 1], blk[c - 1]] if c else []
                if c > 0:
                    a = c - 1
                    b, full = fill(lambda M: [mm(M[par * DH:(par + 1) * DH, g * P:(g + 1) * P],
                                                 AN[:, a % 2, g, par * DH:(par + 1) * DH], BLK[:, a % 2, 2 * g + par, :])
                                              for g in range(QG) for par in range(2)], [an[a], blk[a]])
                    free["AN", a % 2] = [full]
                    free["BLK", a % 2] = [full]
                    if a + 2 < NC:
                        blk.append(mask_blocks(a + 2))
                    n = QG * TK
                    made["OT", a] = drain(b, full, None,
                                          OT[:, :, a * n:(a + 1) * n].rearrange("p e t -> p t e"),
                                          psM[b][:, :].rearrange("p (t e) -> p t e", e=E), free.get("OT", []))
                    yield [an[c], blk[c]] if c == NC - 1 else [made["OT", x] for x in range(NC)] if c == NC else []
            free["MASK", p % 3] = [blk[-1]]
            for n in range(NT):
                b, full = fill(lambda M: [mm(M[:, 0:C], OT[:, e, n * P:(n + 1) * P], wo[:, e, :], e == 0, e == E - 1)
                                          for e in range(E)], [made["OT", a] for a in range(NC)])
                xs = X[:, s % XRING, n, :]
                m = put("dve", lambda e, b=b, xs=xs: e.scalar_tensor_tensor(xs, psM[b][:, 0:C], 0.5, xs, ALU.mult, ALU.add),
                        [full], s_free[b])
                bank_free[b] = [m]
                yield
            free["OT"] = [full]
            x_ready[s] = [m]
            if not attention:
                stored[s] = put("sp", lambda e: e.dma_start(out[s].rearrange("(n p) c -> p n c", p=P), X[:, s % XRING]),
                                [m], s_out, 16)

        def attend(s):
            xs = X[:, s % XRING, :, :].rearrange("p n c -> p (n c)")
            m, = x_ready[s]
            yield from layernorm(1, lambda n: X[:, s % XRING, n, :], lambda n: XN[:, 1, n, :], [m], free.get("XN1", []))
            yield [normed[1]]
            b, full = transpose_tokens(1, lambda n: XN[:, 1, n, :], None)
            free["XN1"] = [full]
            xnt = drain(b, full, None, XNT[:, 1, :], psM[b][:, 0:T], free.get("XNT1", []))
            yield [xnt]
            for n in range(NT):
                b, full = fill(lambda M: [mm(M[:, :], XNT[:, 1, n * P:(n + 1) * P], awkv[:, :])], [xnt, resid])
                kv = put("dve", lambda e, b=b, n=n: e.tensor_tensor(KV[:, n, :], psM[b][:, :], bkv[:, :], ALU.add),
                         [full, *free.get("KV", [])], s_free[b])
                bank_free[b] = [kv]
                yield
            b, full = fill(lambda M: [mm(M[:, 0:T], awq[:, :], XNT[:, 1, :])], [xnt, resid])
            free["XNT1"] = [full]
            aq = put("dve", lambda e, b=b: e.tensor_scalar(AQ[:, :], psM[b][:, 0:T], bq[:, 0:1], None, ALU.add),
                     [full, *free.get("AQ", [])], s_free[b])
            bank_free[b] = [aq]
            yield [kv, aq]
            b, full = fill(lambda M: [mm(M[:, k * C:(k + 1) * C], KV[:, n, k * C:(k + 1) * C], KV[:, n, (2 + k) * C:(3 + k) * C],
                                         n == 0, n == NT - 1) for k in range(2) for n in range(NT)], [kv])
            free["KV"] = [full]
            m = put("dve", lambda e, b=b: e.scalar_tensor_tensor(S0[:, :], psM[b][:, 0:C], SSCALE, headmask[:, :],
                                                                 ALU.mult, ALU.mult), [full], s_dve)
            m = put("dve", lambda e, b=b: e.tensor_tensor(ST[:, :], psM[b][:, C:2 * C], S0[:, :], ALU.mult),
                    [m, *free.get("ST", [])], s_free[b])
            bank_free[b] = [m]
            yield [m]
            b, full = fill(lambda M: [mm(M[:, n * C:(n + 1) * C], AQ[:, n * P:(n + 1) * P], ST[:, :]) for n in range(NT)],
                           [aq, m])
            free["ST"] = free["AQ"] = [full]
            m = drain(b, full, None, AO[:, :, :], psM[b][:, 0:NT * C].rearrange("p (n c) -> p n c", n=NT),
                      free.get("AO", []))
            yield [m]
            yield from layernorm(2, lambda n: AO[:, n, :], lambda n: AON[:, n, :], [m], free.get("AON", []))
            free["AO"] = [normed[2]]
            yield [normed[2]]
            b, full = transpose_tokens(2, lambda n: AON[:, n, :], None)
            free["AON"] = [full]
            m = put("dve", lambda e, b=b: e.tensor_scalar(AOT[:, :], psM[b][:, 0:T], lng[:, 0:1], lnb[:, 0:1], ALU.mult, ALU.add),
                    [full, *free.get("AOT", [])], s_free[b])
            bank_free[b] = [m]
            yield [m]
            b, full = fill(lambda M: [mm(M[:, n * C:(n + 1) * C], AOT[:, n * P:(n + 1) * P], awo[:, :]) for n in range(NT)], [m])
            free["AOT"] = [full]
            m = put("dve", lambda e, b=b: e.tensor_tensor(xs, psM[b][:, 0:NT * C], xs, ALU.add), [full], s_free[b])
            bank_free[b] = [m]
            xn = X[:, s % XRING, :, :]
            m = put("pool", lambda e: e.tensor_tensor(xn, xn, bo[:, :].unsqueeze(1).to_broadcast([P, NT, C]), ALU.add),
                    [m], s_pool)
            x_ready[s] = [m]

        score_free = [[], []]
        pt_free = [[], []]
        o_free = []
        pb_free = [[] for _ in range(3)]
        ptb_free = [[] for _ in range(4)]
        maxed, copied = {}, {}

        exped = {}

        def scores(n):
            p, h = divmod(n, H)
            par, r, c, j = h % 2, n % 4, n // (2 * CH), h // 2 % CH
            ring, own = c % QRING, slice(par * DH, par * DH + DH)
            for it in range(NT):
                q = QS[:, ring, j, par, it * P:(it + 1) * P]
                put("pe", lambda e, it=it, q=q: e.matmul(psS[n % 2][:, it, :], q, KS[:, ring, j, par, :], start=True, stop=False),
                    [*made["Q", c], *made["K", c], *score_free[n % 2]] if it == 0 else ())
                m = put("pe", lambda e, it=it, q=q: e.matmul(psS[n % 2][:, it, :], q[own], KL[own, ring, j, :], start=False, stop=True),
                        (), s_score if it == NT - 1 else None, ns=110)
            if h % (2 * CH) == 2 * CH - 1:
                free["QK", ring] = [m]
            maxed[n] = put("dve", lambda e: e.tensor_reduce(NMAX[:, r, :], psS[n % 2][:, :, :], AX_X, ALU.max, negate=True),
                           [m], s_max, ns=600)

        def exponentials(n):
            p, h = divmod(n, H)
            r, o, par, hp = n % 4, p % 2, h % 2, h // 2
            for it in range(NT):
                m = put("act", lambda e, it=it: e.activation(PB[:, n % 3, it, :], psS[n % 2][:, it, :], ACT.Exp,
                                                            bias=NMAX[:, r, it:it + 1],
                                                            accum_out=SUM[:, o, it, par, hp:hp + 1]),
                        [maxed[n], *pb_free[n % 3], *free.get(("SUM", o), [])], s_exp, ns=450)
            made["SUM", p] = m
            score_free[n % 2] = exped[n] = [m]

        def turn(n):
            steps = [tr(psT[n % 2][:, jt, it * P:(it + 1) * P], PB[:, n % 3, it, jt * P:(jt + 1) * P])
                     for it in range(NT) for jt in range(NT)]
            for k, step in enumerate(steps):
                m = put("pe", step, [*exped[n], *pt_free[n % 2]] if k == 0 else (), s_pt if k == 3 else None, ns=110)
            pb_free[n % 3] = [m]
            m = copy(None, PT[:, n % 4, :, :], psT[n % 2][:, :, :], [m, *ptb_free[n % 4]], s_ptc[n % 2])
            pt_free[n % 2] = [m]
            copied[n] = m

        def product(n):
            p, h = divmod(n, H)
            o, hp = p % 2, h // 2
            vs = [made["V", p, 2 * jt + hp // 4] for jt in range(NT)]
            for jt in range(NT):
                for par in range(2):
                    first = jt == par == 0
                    last = jt == NT - 1 and par == 1
                    m = put("pe", mm(psO[par * DH:(par + 1) * DH, :], V[:, o, jt, hp, par * DH:(par + 1) * DH],
                                     PT[:, (n + par) % 4, jt, :], jt == 0, jt == NT - 1),
                            [copied[n], copied[n + 1], *vs, *o_free] if first else (), s_pv if last else None, ns=215)
            ptb_free[n % 4] = ptb_free[(n + 1) % 4] = [m]
            if h == H - 2:
                free["V", o] = [m]
            m = copy(None, AT[:, o, :, hp], psO[:, :], [m, *free.get(("AT", o), [])], s_oc)
            o_free[:] = [m]
            made["AT", p] = m


        order = [(s, True) for s in range(min(LEAD, NSEQ))]
        for s in range(NSEQ):
            order.append((s, False))
            if s + LEAD < NSEQ:
                order.append((s + LEAD, True))
        if NSEQ < LEAD:
            raise ValueError("too few sequences")

        for first in (norm(0, order[0][0]), prologue(0), choose(0), values(0), norm(1, order[1][0])):
            for _ in first:
                pass
        total = len(order) * H
        for c in range(2):
            for k in range(2):
                project(c, k)
        scores(0)
        exponentials(0)
        def finish(kind):
            for w in stages:
                if w.kind == kind:
                    w.finish()

        def background(now, until=0.0):
            while True:
                able = [w for w in stages if not w.done and w.ready() <= clock["pe"] + SLACK]
                due = [w for w in able if w.due(now)]
                if due:
                    min(due, key=lambda w: w.ready()).step()
                elif able and clock["pe"] + EAGER < until:
                    min(able, key=lambda w: w.at - w.size * (now - w.start) / (w.end - w.start)).step()
                else:
                    return

        def begin(kind, steps, n):
            first, last = SPANS[kind]
            stages.append(Background(steps, kind, n, n + last - first))

        for n in range(total + TLAG + 3):
            p, h = divmod(n, H)
            more = p + 1 < len(order)
            if h == SPANS["prologue"][0] and more:
                begin("prologue", prologue(p + 1), n)
            if h == SPANS["choose"][0] and more:
                finish("prologue")
                begin("choose", choose(p + 1), n)
            if h == SPANS["values"][0] and more:
                finish("choose")
                begin("values", values(p + 1), n)
            if h == SPANS["attend"][0] and 2 <= p and order[p - 2][1]:
                begin("attend", attend(order[p - 2][0]), n)
            if h == SPANS["norm"][0] and p + 2 < len(order):
                finish("attend")
                begin("norm", norm(p + 2, order[p + 2][0]), n)
            if h == SPANS["epilogue"][0] and 0 < p < len(order):
                begin("epilogue", epilogue(p - 1, *order[p - 1]), n)
            if (n + 1) % H == 0:
                for w in stages:
                    if w.kind != "epilogue" and w.kind != "norm" and w.kind != "values":
                        w.finish()
            for k, what in enumerate(TURN):
                until = 0.0
                if what == "S" and n + 1 < total:
                    until = ready_at(score_free[(n + 1) % 2])
                if what == "T" and TLAG <= n < total + TLAG:
                    until = ready_at([*exped[n - TLAG], *pt_free[(n - TLAG) % 2]])
                if what == "P" and n >= TLAG + 2 and (n - TLAG) % 2 == 0 and n - TLAG - 2 < total:
                    until = ready_at([copied[n - TLAG - 1], *o_free])
                background(n + k / len(TURN), until)
                if what == "S" and n + 1 < total:
                    scores(n + 1)
                c, phase = divmod(n + PLEAD, 2 * CH)
                if what == "C" and 2 <= c < total // (2 * CH) and phase < 2:
                    project(c, phase)
                if what == "E" and n + 1 < total:
                    exponentials(n + 1)
                if what == "T" and TLAG <= n < total + TLAG:
                    turn(n - TLAG)
                if what == "P" and n >= TLAG + 2 and (n - TLAG) % 2 == 0 and n - TLAG - 2 < total:
                    product(n - TLAG - 2)
            if (n + 1) % H == 0:
                for w in stages:
                    w.finish()
                stages.clear()
        begin("epilogue", epilogue(len(order) - 1, *order[-1]), total)
        for w in stages:
            w.finish()
        queue["sp"].append(("wait", s_out, count[s_out]))

        block = ctx.enter_context(nc.Block())

        @block.sync
        def _(eng):
            play("sp", eng)

        @block.tensor
        def _(eng):
            play("pe", eng)

        @block.vector
        def _(eng):
            play("dve", eng)

        @block.scalar
        def _(eng):
            play("act", eng)

        @block.gpsimd
        def _(eng):
            play("pool", eng)


def kernel(**inputs):
    import numpy as np
    import concourse.bacc as bacc
    from concourse.bass_utils import run_bass_kernel_spmd

    a = {k: np.asarray(v) for k, v in inputs.items()}
    x = a["L0_attn_x"]
    n, t, c = x.shape
    h, dh = a["L0_ffn_Wq"].shape[:2]
    e = a["L0_ffn_Wv"].shape[0]
    head = 8
    one = np.float32(1)
    row, col = np.arange(P)[:, None], np.arange(P)[None, :]
    arrays = {
        "x": x,
        "WqT": a["L0_ffn_Wq"].reshape(h * dh, c).T,
        "WkT": a["L0_ffn_Wk"].reshape(h * dh, c).T,
        "WvT": a["L0_ffn_Wv"].reshape(e * dh, c).T,
        "WgT": np.concatenate([a["L0_ffn_Ws"], a["L0_ffn_Wd"]], axis=1).reshape(h * 2 * e, c).T,
        "WoT": a["L0_ffn_Wo"].transpose(2, 0, 1),
        "aWq": a["L0_attn_Wq"],
        "aWkv": np.concatenate([*a["L0_attn_Wk"], *a["L0_attn_Wv"]], axis=1),
        "aWo": a["L0_attn_Wo"],
        "b_q": a["L0_attn_bq"],
        "b_kv": np.concatenate([*a["L0_attn_bk"], *a["L0_attn_bv"]]),
        "b_o": a["L0_attn_bo"],
        "ln_g": a["L0_attn_ln_g"],
        "ln_b": a["L0_attn_ln_b"],
        "ident": np.where(row == col, one, 0 * one),
        "order": (lambda r: np.where(((r // 64) * 64 + (r % 4) * 16 + (r // 4 % 4) * 4 + r // 16 % 4) == col, one, 0 * one))(row),
        "delta": np.where(row // 8 == col // 8, one, 0 * one),
        "token": np.where(row % TK == col // (P // TK), one, 0 * one),
        "group": np.where(row // TK == np.arange(P // TK)[None, :], one, 0 * one),
        "ramp": np.broadcast_to(np.arange(e, 0, -1, dtype=np.float32), (P, e)),
        "heads": np.where(row // head == col // head, one, 0 * one),
    }
    arrays = {k: np.ascontiguousarray(v) for k, v in arrays.items()}
    nc = bacc.Bacc("TRN2", target_bir_lowering=False, num_devices=1)
    args = [nc.dram_tensor(f"in_{k}", v.shape, mybir.dt.from_np(v.dtype), kind="ExternalInput").ap()
            for k, v in arrays.items()]
    out = nc.dram_tensor("out", x.shape, F32, kind="ExternalOutput").ap()
    macaron_kernel(nc, *args, out)
    r = run_bass_kernel_spmd(nc, [{f"in_{k}": v for k, v in arrays.items()}], core_ids=[0])
    return r.results[0]["out"]
```
